# Optimizing a Trainium2 kernel written in Bass

```python
import numpy as np
import jax
import jax.numpy as jnp

def _softmax(x, axis=-1):
    return jax.nn.softmax(x, axis=axis)

def _gelu(x):
    return jax.nn.gelu(x, approximate=True)

def _silu(x):
    return jax.nn.silu(x)

def _sigmoid(x):
    return jax.nn.sigmoid(x)

def _layernorm(x, axis=-1, eps=1e-05):
    m = jnp.mean(x, axis=axis, keepdims=True)
    v = jnp.var(x, axis=axis, keepdims=True)
    return (x - m) / jnp.sqrt(v + eps)

def _scatter_add(tgt, idx, src, axis=0):
    return tgt.at[idx].add(src)

def _segment_sum(src, seg, n):
    return jax.ops.segment_sum(src, seg, n)
kernel_name = 'mk_flamingo_gated_d1_seqx_r8_480754'

def setup_inputs(seed: int=0):
    np.random.seed(seed)
    _w = jnp.asarray

    def _rec_inputs():
        import jax
        import jax.numpy as jnp
        _rk = jax.random.key(seed)
        x = 7.22e-05 + 1 * jax.random.normal(jax.random.fold_in(_rk, 1), (2, 256, 128), jnp.float32)
        _lenS = 256 - jax.random.randint(jax.random.fold_in(_rk, 7), (2,), 0, max(1, 256 // 4) + 1, jnp.int32)
        _lenS2 = 512 - jax.random.randint(jax.random.fold_in(_rk, 8), (2,), 0, max(1, 512 // 4) + 1, jnp.int32)
        _ctx_1024P = jax.random.normal(jax.random.fold_in(_rk, 11), (2, 16, 128), jnp.float32)
        _ctx_1024c = jax.random.dirichlet(jax.random.fold_in(_rk, 511), 0.3 * jnp.ones((16,), jnp.float32), (2, 512))
        _ctx_1024t = jnp.einsum('bsk,bkd->bsd', _ctx_1024c, _ctx_1024P)
        _ctx_1024t = _ctx_1024t * jax.lax.rsqrt(jnp.mean(jnp.square(_ctx_1024t)) + 1e-12) * 0.953939
        ctx_1024 = 4.13588e-05 + 0.999923 * (_ctx_1024t + 0.3 * jax.random.normal(jax.random.fold_in(_rk, 611), (2, 512, 128), jnp.float32))
        _g = jax.random.normal(jax.random.fold_in(_rk, 9001), (2, 1), jnp.float32)
        _g = jnp.sign(_g) * jnp.maximum(jnp.abs(_g), 1.0) + (_g == 0) * 1.0
        g_xattn = _g[0]
        g_ffn = _g[1]
        return (x, ctx_1024, g_xattn, g_ffn)
    x, ctx_1024, g_xattn, g_ffn = _rec_inputs()

    def _L0_xattn_setup():
        import jax, jax.numpy as jnp
        import numpy as np
        HEADS = 8
        DIM_HEAD = 64
        key = jax.random.key(seed)
        ks = jax.random.split(key, 9)
        B, N1, N2, D = (4, 256, 256, 128)
        inner = HEADS * DIM_HEAD
        s_in = 1.0 / np.sqrt(D)
        s_inner = 1.0 / np.sqrt(inner)
        return {'x1': jax.random.normal(ks[0], (B, N1, D), jnp.float32), 'x2': jax.random.normal(ks[1], (B, N2, D), jnp.float32), 'Wq1': jax.random.normal(ks[2], (D, inner), jnp.float32) * s_in, 'Wk1': jax.random.normal(ks[3], (D, inner), jnp.float32) * s_in, 'Wv1': jax.random.normal(ks[4], (D, inner), jnp.float32) * s_in, 'Wk2': jax.random.normal(ks[5], (D, inner), jnp.float32) * s_in, 'Wv2': jax.random.normal(ks[6], (D, inner), jnp.float32) * s_in, 'Wo': jax.random.normal(ks[7], (inner, D), jnp.float32) * s_inner, 'bo': jnp.zeros((D,), jnp.float32)}
    _L0_xattn_all = _L0_xattn_setup()
    _L0_xattn_in = {k: v for k, v in _L0_xattn_all.items() if k in ('Wq1', 'Wk1', 'Wv1', 'Wk2', 'Wv2', 'Wo', 'bo')}
    del _L0_xattn_all

    def _L0_ffn_setup():
        import jax, jax.numpy as jnp
        import numpy as np
        B, S, DIM = (4, 256, 128)
        E, K, HID = (8, 2, 512)
        key = jax.random.key(seed)
        ks = jax.random.split(key, 8)
        init = lambda k, sh: jax.random.normal(k, sh, jnp.float32) * 0.02
        return {'x': jax.random.normal(ks[0], (B, S, DIM), jnp.float32), 'gate_w': init(ks[1], (DIM, E)), 'gate_b': jnp.zeros((E,), jnp.float32), 'w1': init(ks[2], (E, DIM, HID)), 'b1': jnp.zeros((E, HID), jnp.float32), 'w2': init(ks[3], (E, HID, DIM)), 'b2': jnp.zeros((E, DIM), jnp.float32), 'ws1': init(ks[4], (DIM, HID)), 'bs1': jnp.zeros((HID,), jnp.float32), 'ws2': init(ks[5], (HID, DIM)), 'bs2': jnp.zeros((DIM,), jnp.float32)}
    _L0_ffn_all = _L0_ffn_setup()
    _L0_ffn_in = {k: v for k, v in _L0_ffn_all.items() if k in ('gate_w', 'gate_b', 'w1', 'b1', 'w2', 'b2', 'ws1', 'bs1', 'ws2', 'bs2')}
    del _L0_ffn_all
    return {'x': x, 'ctx_1024': ctx_1024, 'g_xattn': g_xattn, 'g_ffn': g_ffn, 'L0_xattn_Wq1': _L0_xattn_in['Wq1'], 'L0_xattn_Wk1': _L0_xattn_in['Wk1'], 'L0_xattn_Wv1': _L0_xattn_in['Wv1'], 'L0_xattn_Wk2': _L0_xattn_in['Wk2'], 'L0_xattn_Wv2': _L0_xattn_in['Wv2'], 'L0_xattn_Wo': _L0_xattn_in['Wo'], 'L0_xattn_bo': _L0_xattn_in['bo'], 'L0_ffn_gate_w': _L0_ffn_in['gate_w'], 'L0_ffn_gate_b': _L0_ffn_in['gate_b'], 'L0_ffn_w1': _L0_ffn_in['w1'], 'L0_ffn_b1': _L0_ffn_in['b1'], 'L0_ffn_w2': _L0_ffn_in['w2'], 'L0_ffn_b2': _L0_ffn_in['b2'], 'L0_ffn_ws1': _L0_ffn_in['ws1'], 'L0_ffn_bs1': _L0_ffn_in['bs1'], 'L0_ffn_ws2': _L0_ffn_in['ws2'], 'L0_ffn_bs2': _L0_ffn_in['bs2']}

def reference(x, ctx_1024, g_xattn, g_ffn, L0_xattn_Wq1, L0_xattn_Wk1, L0_xattn_Wv1, L0_xattn_Wk2, L0_xattn_Wv2, L0_xattn_Wo, L0_xattn_bo, L0_ffn_gate_w, L0_ffn_gate_b, L0_ffn_w1, L0_ffn_b1, L0_ffn_w2, L0_ffn_b2, L0_ffn_ws1, L0_ffn_bs1, L0_ffn_ws2, L0_ffn_bs2):
    import jax
    import jax.numpy as jnp

    def _L0_xattn_ref(x1, x2, Wq1, Wk1, Wv1, Wk2, Wv2, Wo, bo):
        import jax, jax.numpy as jnp
        import numpy as np
        HEADS = 8
        DIM_HEAD = 64
        h, d = (HEADS, DIM_HEAD)
        scale = d ** (-0.5)
        B, N1, _ = x1.shape
        N2 = x2.shape[1]

        def split_heads(t, n):
            return t.reshape(B, n, h, d)
        q1 = split_heads(x1 @ Wq1, N1)
        k1 = split_heads(x1 @ Wk1, N1)
        v1 = split_heads(x1 @ Wv1, N1)
        k2 = split_heads(x2 @ Wk2, N2)
        v2 = split_heads(x2 @ Wv2, N2)
        k = jnp.concatenate([k1, k2], axis=1)
        v = jnp.concatenate([v1, v2], axis=1)
        sim = jnp.einsum('bihd,bjhd->bhij', q1.astype(jnp.float32), k.astype(jnp.float32)) * scale
        attn = jax.nn.softmax(sim, axis=-1)
        out = jnp.einsum('bhij,bjhd->bihd', attn, v)
        out = out.reshape(B, N1, h * d)
        return out @ Wo + bo

    def _L0_ffn_ref(x, gate_w, gate_b, w1, b1, w2, b2, ws1, bs1, ws2, bs2):
        import jax, jax.numpy as jnp
        import numpy as np
        B, S, DIM = (4, 256, 128)
        E, K, HID = (8, 2, 512)
        orig_shape = x.shape
        xf = x.reshape(-1, DIM)
        logits = xf @ gate_w + gate_b
        top_w, top_i = jax.lax.top_k(logits, K)
        gw = jax.nn.softmax(top_w, axis=-1).astype(xf.dtype)
        combine = (gw[:, :, None] * jax.nn.one_hot(top_i, E, dtype=xf.dtype)).sum(axis=1)
        out = jnp.zeros_like(xf)
        for e in range(E):
            h = jax.nn.gelu(xf @ w1[e] + b1[e], approximate=False)
            out = out + combine[:, e:e + 1] * (h @ w2[e] + b2[e])
        shared = jax.nn.gelu(xf @ ws1 + bs1, approximate=False) @ ws2 + bs2
        return (out + shared).reshape(orig_shape)
    x = x + jnp.tanh(g_xattn[0]) * _L0_xattn_ref(_layernorm(x, axis=-1), ctx_1024, L0_xattn_Wq1, L0_xattn_Wk1, L0_xattn_Wv1, L0_xattn_Wk2, L0_xattn_Wv2, L0_xattn_Wo, L0_xattn_bo)
    x = x + jnp.tanh(g_ffn[0]) * _L0_ffn_ref(_layernorm(x, axis=-1), L0_ffn_gate_w, L0_ffn_gate_b, L0_ffn_w1, L0_ffn_b1, L0_ffn_w2, L0_ffn_b2, L0_ffn_ws1, L0_ffn_bs1, L0_ffn_ws2, L0_ffn_bs2)
    return x

_drawn_inputs = setup_inputs


def setup_inputs(seed=0):
    import zlib

    import numpy as np

    out = dict(_drawn_inputs(seed))
    spreads = {'L0_xattn_bo': (0.0, 0.1),
     'L0_ffn_gate_b': (0.0, 0.1),
     'L0_ffn_b1': (0.0, 0.534),
     'L0_ffn_b2': (0.0, 0.1),
     'L0_ffn_bs1': (0.0, 0.409),
     'L0_ffn_bs2': (0.0, 0.1)}
    factors = {}
    for name, (base, spread) in spreads.items():
        noise = np.random.default_rng([zlib.crc32(name.encode()), seed]).standard_normal(out[name].shape)
        drawn = base * np.exp(spread * noise) if base else spread * noise
        out[name] = jnp.asarray(drawn.astype(out[name].dtype))
    for name, factor in factors.items():
        out[name] = (out[name] * factor).astype(out[name].dtype)
    return out
```

```python
from contextlib import ExitStack
from math import log

import concourse.bass as bass
from concourse import mybir

F32 = mybir.dt.float32
F16 = mybir.dt.float16
ALU = mybir.AluOpType
ACT = mybir.ActivationFunctionType
AX_X = mybir.AxisListType.X

P = 128
B = 2
T1 = 256
T2 = 512
D = 128
HEADS = 8
DH = 64
INNER = HEADS * DH
PAIRS = HEADS // 2
KEYS = T1 + T2
KT = KEYS // P
QT = T1 // P
NT = B * QT
NH = B * HEADS
E = 8
NE = E + 1
HID = 512
HC = HID // P
NW = 6
WK2, WK1, WQ, WV2, WV1, WO = range(NW)
RING = 4
EORDER = [E] + list(range(E))
EPS = 1e-5

S_ACTV = 64.0
S_W = 1024.0
S_SCORE = S_ACTV * S_ACTV
SHIFT_ROW = S_SCORE
P_SCALE = S_ACTV
SHIFT_P = log(P_SCALE) * DH ** 0.5
NONE = -3.0e38
PICKED = 3.0e38

ST_LAG = 2
HI_LAG = 3
PV_LAG = 4
NORM_LAG = 5
FFN0 = NH + ST_LAG
NF = B * NE
STEPS = FFN0 + NF + 4
TAIL0 = [HEADS - 1 + NORM_LAG, NH - 1 + NORM_LAG]
BIAS_STEP = 10
FSPLIT0 = 14
(TAIL_O0, TAIL_O1, TAIL_WO, TAIL_X, TAIL_GATE, TAIL_COMB, TAIL_B2) = range(7)


def tail_of(i):
    return [(b, i - TAIL0[b]) for b in range(B) if 0 <= i - TAIL0[b] <= TAIL_B2]


def plan_items():
    items = [("tx", 0), ("tc", 0)]
    items += [("k", 0, p) for p in range(PAIRS)]
    items += [("q", p) for p in range(PAIRS)]
    items += [("tc", 1)]
    items += [("v", 0, t) for t in range(KT)]
    items += [("k", 1, p) for p in range(PAIRS)]
    items += [("v", 1, t) for t in range(KT)]
    return items


ITEMS = plan_items()
NI = len(ITEMS)
SPLIT_BEFORE = {1: [WK2], 2: [WK1], 3: [WQ], 6: [WV2], 10: [WV1], 14: [WO]}
SPLIT_ORDER = [w for n in sorted(SPLIT_BEFORE) for w in SPLIT_BEFORE[n]]
SPLIT_AT = {w: SPLIT_ORDER.index(w) + 1 for w in SPLIT_ORDER}


def plan_misc():
    uses = []
    for i in range(STEPS):
        if 1 <= i <= NH:
            uses.append(("shift", i - 1))
        if i == BIAS_STEP:
            uses.append(("b1", 0))
        for b, s in tail_of(i):
            uses.append((s, b))
    return {u: n for n, u in enumerate(uses)}


MISC = plan_misc()


def block_kernel(nc, x, ctx_in, g_xattn, g_ffn, Wq1, Wk1, Wv1, Wk2, Wv2, Wo, bo,
                 gate_w, gate_b, w1, b1, w2, b2, ws1, bs1, ws2, bs2, out):
    stack = ExitStack()
    with stack:
        def sb(name, shape, dt):
            return stack.enter_context(nc.sbuf_tensor(name, shape, dt))

        def sem(name):
            return stack.enter_context(nc.semaphore(name))

        x_sb = sb("x_sb", [P, NT, D], F32)
        early = sb("early", [P, B * T2 // P * D + 512], F32)
        ctx_sb = early[:, 0:B * T2 // P * D].rearrange("p (t d) -> p t d", d=D)
        prob = early[:, 0:2 * (KEYS // 2) * QT].rearrange("p (g n) -> p g n", g=2)
        xT = sb("xT", [P, 2, B * T1], F16)
        cT = sb("cT", [P, 2, B * T2], F16)
        ring = sb("ring", [P, RING, 2, 512], F32)
        wa = sb("wa", [P, 2, NW, 512], F16)
        wf = sb("wf", [P, 2, NE, 2, 512], F16)
        kab = sb("kab", [P, 2, HEADS, KEYS], F16)
        k_a = kab[:, 0]
        k_b = kab[:, 1]
        kflat = kab[:, :, :, :].rearrange("p a h n -> p (a h n)")
        hid = kflat[:, 0:4096].bitcast(F32).rearrange("p (u n) -> p u n", u=2)
        hid_hi = kflat[:, 4096:6144].rearrange("p (u n) -> p u n", u=2)
        hid_lo = kflat[:, 6144:8192].rearrange("p (u n) -> p u n", u=2)
        k_nat = sb("k_nat", [P, 2, PAIRS, KEYS], F16)
        q_a = sb("q_a", [P, HEADS, B * T1], F16)
        q_b = sb("q_b", [P, HEADS, B * T1], F16)
        qo = sb("qo", [P, 2, 4, 512], F16)
        q_nat = qo
        oT = qo
        v_hi = sb("v_hi", [P, B * KT, HEADS, DH + 1], F16)
        v_lo = sb("v_lo", [P, B * KT, HEADS, DH], F16)
        p_hi = sb("p_hi", [P, 3, KT, T1], F16)
        p_lo = sb("p_lo", [P, 3, KT, T1], F16)
        o_sb = sb("o_sb", [P, NT, INNER], F32)
        xn = sb("xn", [P, NT, D], F32)
        acc = sb("acc", [P, NT, D], F32)
        x2T = sb("x2T", [P, NT * P], F32)
        x2h = sb("x2h", [P, 2, NT * P], F16)
        ident = sb("ident", [P, P], F32)
        ident16 = sb("ident16", [P, P], F16)
        b1_rows = sb("b1_rows", [NE * HC, P], F32)
        b1T = sb("b1T", [P, NE * HC], F32)
        b2_rows = sb("b2_rows", [NE, D], F32)
        gw = sb("gw", [P, E], F32)
        gb = sb("gb", [P, E], F32)
        bo_sb = sb("bo_sb", [P, D], F32)
        gates = sb("gates", [P, 4], F32)
        scales = sb("scales", [P, 2], F32)
        nmax = sb("nmax", [P, NH, QT], F32)
        shift16 = sb("shift16", [P, NH, QT], F16)
        rsum = sb("rsum", [P, NH, QT], F32)
        stats = sb("stats", [P, 2 * NT, 6], F32)
        mv = sb("mv", [P, 2 * NT, 2], F32)
        vare = sb("vare", [P, 2 * NT], F32)
        rstd = sb("rstd", [P, 2 * NT], F32)
        c_mhalf = sb("c_mhalf", [P, 2 * NT], F32)
        c_e = sb("c_e", [P, QT, E], F32)
        logit = sb("logit", [P, NT, 2 * E], F32)
        top8 = sb("top8", [P, NT, 8], F32)
        pick8 = sb("pick8", [P, NT, 8], F32)
        marked = sb("marked", [P, NT, 2 * E], F32)
        mask = sb("mask", [P, NT, E], F32)
        diff = sb("diff", [P, NT, E], F32)
        gexp = sb("gexp", [P, NT, E], F32)
        gsum = sb("gsum", [P, NT], F32)
        grec = sb("grec", [P, NT], F32)
        comb = sb("comb", [P, NT, NE], F32)
        comb_s = sb("comb_s", [P, NT, NE], F32)
        combT = sb("combT", [NE, NT * P], F32)

        banks = stack.enter_context(nc.psum_tensor("banks", [P, 8, 512], F32))

        def span(first, n):
            return banks[:, first:first + 2, :].rearrange("p a n -> p (a n)")[:, 0:n]

        o_ps = banks[:, 6, 0:QT * (DH + 1)].rearrange("p (q d) -> p q d", q=QT)
        misc = banks[:, 7, :]

        ld_x, ld_small, ld_rows = sem("ld_x"), sem("ld_small"), sem("ld_rows")
        ld_ctx = [sem(f"ld_ctx{b}") for b in range(B)]
        ld_w = [sem(f"ld_w{w}") for w in range(NW)]
        ld_f = [sem(f"ld_f{j}") for j in range(NE)]
        consts = sem("consts")
        pool_chain = sem("pool_chain")
        dve_chain = sem("dve_chain")
        var_ready = sem("var_ready")
        rstd_ready = sem("rstd_ready")
        xn_ready = sem("xn_ready")
        tanh_done = sem("tanh_done")
        xb_done = sem("xb_done")
        w_hi, w_lo = sem("w_hi"), sem("w_lo")
        item_ps = sem("item_ps")
        item_hi, item_lo = sem("item_hi"), sem("item_lo")
        k_st = [sem(f"k_st{n}") for n in range(B * PAIRS)]
        q_st = [sem(f"q_st{n}") for n in range(PAIRS)]
        max_ps = sem("max_ps")
        max_done = sem("max_done")
        shift_ready = sem("shift_ready")
        score_ps = sem("score_ps")
        exp_done = sem("exp_done")
        ph_act, ph_dve = sem("ph_act"), sem("ph_dve")
        pl_done = sem("pl_done")
        pv_ps = sem("pv_ps")
        o_done = sem("o_done")
        misc_ps = sem("misc_ps")
        misc_hi = sem("misc_hi")
        misc_done = sem("misc_done")
        gexp_go, gexp_done = sem("gexp_go"), sem("gexp_done")
        comb_ready = sem("comb_ready")
        f_hi, f_lo = sem("f_hi"), sem("f_lo")
        h_ps = sem("h_ps")
        gelu_done = sem("gelu_done")
        hh_done, hl_done = sem("hh_done"), sem("hl_done")
        y_ps = sem("y_ps")
        y_done = sem("y_done")
        stored = sem("stored")

        x_d = x.rearrange("b (t p) d -> p (b t) d", p=P)
        ctx_d = ctx_in.rearrange("b (t p) d -> b p t d", p=P)
        out_d = out.rearrange("b (t p) d -> b p t d", p=P)
        w_d = {WK2: Wk2, WK1: Wk1, WQ: Wq1, WV2: Wv2, WV1: Wv1}

        def ring_a(w):
            n = SPLIT_AT[w] - 1
            return ring[:, n // 2, n % 2, :]

        def ring_f(j):
            return ring[:, (3 + j) % RING]

        def ctx_cols(b, t):
            return slice(b * T2 + t * P, b * T2 + (t + 1) * P)

        def item_out(n):
            kind = ITEMS[n][0]
            return span(2 * (n % 4), KEYS if kind == "k" else 512)

        block = stack.enter_context(nc.Block())

        @block.sync
        def _(sp):
            def load_a(w):
                dst = ring_a(w)
                if w == WO:
                    sp.dma_start(dst.rearrange("p (c n) -> p c n", n=D),
                                 Wo.rearrange("(c p) n -> p c n", p=P)).then_inc(ld_w[w], 16)
                else:
                    sp.dma_start(dst, w_d[w]).then_inc(ld_w[w], 16)

            def load_f(j):
                e = EORDER[j]
                slot = ring_f(j)
                src1, src2 = (ws1, ws2) if e == E else (w1[e], w2[e])
                if 1 <= j < RING:
                    sp.wait_ge(w_lo, 2 * j)
                elif j >= RING:
                    sp.wait_ge(f_lo, j - RING + 1)
                sp.dma_start(slot[:, 0, :], src1).then_inc(ld_f[j], 16)
                sp.dma_start(slot[:, 1, :].rearrange("p (c n) -> p c n", n=D),
                             src2.rearrange("(c p) n -> p c n", p=P)).then_inc(ld_f[j], 16)

            sp.dma_start(x_sb[:, :, :], x_d).then_inc(ld_x, 16)
            sp.dma_start(ctx_sb[:, 0:T2 // P, :], ctx_d[0]).then_inc(ld_ctx[0], 16)
            for w in (WK2, WK1, WQ):
                load_a(w)
            sp.dma_start(ctx_sb[:, T2 // P:, :], ctx_d[1]).then_inc(ld_ctx[1], 16)
            for w in (WV2, WV1, WO):
                load_a(w)
            sp.dma_start(gates[:, 0:1], g_xattn.partition_broadcast(P)).then_inc(ld_small, 16)
            sp.dma_start(gates[:, 1:2], g_ffn.partition_broadcast(P)).then_inc(ld_small, 16)
            sp.dma_start(bo_sb[:, :], bo.partition_broadcast(P)).then_inc(ld_small, 16)
            sp.dma_start(gb[:, :], gate_b.partition_broadcast(P)).then_inc(ld_rows, 16)
            sp.dma_start(gw[:, :], gate_w).then_inc(ld_rows, 16)
            sp.dma_start(b1_rows[0:E * HC, :], b1.rearrange("e (c p) -> (e c) p", p=P)).then_inc(ld_rows, 16)
            sp.dma_start(b1_rows[E * HC:, :], bs1.rearrange("(c p) -> c p", p=P)).then_inc(ld_rows, 16)
            sp.dma_start(b2_rows[0:E, :], b2).then_inc(ld_rows, 16)
            sp.dma_start(b2_rows[E:, :], bs2.rearrange("(a n) -> a n", a=1)).then_inc(ld_rows, 16)

            def stack_k(b, p):
                n = b * PAIRS + p
                sp.wait_ge(item_lo, ITEMS.index(("k", b, p)) + 1)
                if b > 0:
                    sp.wait_ge(score_ps, 2 * (2 * p + 2))
                for half in range(2):
                    src = slice(DH * half, DH * half + DH)
                    h = 2 * p + half
                    sp.dma_start(k_a[0:DH, h, :], k_nat[src, 0, p, :]).then_inc(k_st[n], 16)
                    sp.dma_start(k_a[DH:P, h, :], k_nat[src, 1, p, :]).then_inc(k_st[n], 16)
                    sp.dma_start(k_b[0:DH, h, :], k_nat[src, 0, p, :]).then_inc(k_st[n], 16)

            def stack_q(p):
                sp.wait_ge(item_lo, ITEMS.index(("q", p)) + 1)
                for half in range(2):
                    src = slice(DH * half, DH * half + DH)
                    h = 2 * p + half
                    sp.dma_start(q_a[0:DH, h, :], q_nat[src, 0, p, :]).then_inc(q_st[p], 16)
                    sp.dma_start(q_a[DH:P, h, :], q_nat[src, 0, p, :]).then_inc(q_st[p], 16)
                    sp.dma_start(q_b[0:DH, h, :], q_nat[src, 1, p, :]).then_inc(q_st[p], 16)

            for p in range(PAIRS):
                stack_k(0, p)
            for p in range(PAIRS):
                stack_q(p)
            for j in range(RING):
                load_f(j)
            for p in range(PAIRS):
                stack_k(1, p)
            for j in range(RING, NE):
                load_f(j)
            for b in range(B):
                sp.wait_ge(y_done, NE * (b + 1))
                sp.dma_start(out_d[b], acc[:, QT * b:QT * b + QT, :]).then_inc(stored, 16)
            sp.wait_ge(stored, 16 * B)

        @block.gpsimd
        def _(pool):
            n = 0

            def link(ins):
                nonlocal n
                n += 1
                ins.then_inc(pool_chain, 1)
                pool.wait_ge(pool_chain, n)

            nc.gpsimd.memset(c_mhalf[:, :], -0.5).then_inc(consts, 1)
            link(nc.gpsimd.memset(ident[:, :], 0.0))
            nc.gpsimd.affine_select(out=ident[:, :], in_=ident[:, :], compare_op=ALU.not_equal, fill=1.0,
                                    base=0, pattern=[[-1, P]], channel_multiplier=1).then_inc(consts, 1)
            link(nc.gpsimd.memset(ident16[:, :], 0.0))
            nc.gpsimd.affine_select(out=ident16[:, :], in_=ident16[:, :], compare_op=ALU.not_equal, fill=1.0,
                                    base=0, pattern=[[-1, P]], channel_multiplier=1).then_inc(consts, 1)
            pool.wait_ge(consts, 1)
            pool.wait_ge(var_ready, 1)
            nc.gpsimd.tensor_tensor(rstd[:, 0:NT], vare[:, 0:NT], c_mhalf[:, 0:NT], ALU.pow).then_inc(rstd_ready, 1)
            pool.wait_ge(rstd_ready, 1)
            nc.gpsimd.memset(k_b[DH:DH + 1, :, :], SHIFT_ROW).then_inc(consts, 1)
            pool.wait_ge(consts, 4)
            nc.gpsimd.memset(v_hi[:, :, :, DH:DH + 1], S_ACTV).then_inc(consts, 1)
            link(nc.gpsimd.memset(c_e[:, :, :], 2.718281828459045))
            nc.gpsimd.memset(logit[:, :, :], NONE).then_inc(consts, 1)
            nc.gpsimd.memset(pick8[:, :, :], NONE).then_inc(consts, 1)
            nc.gpsimd.memset(comb[:, :, :], 1.0).then_inc(consts, 1)
            pool.wait_ge(tanh_done, 1)
            pool.wait_ge(ld_small, 48)
            link(nc.gpsimd.tensor_scalar(bo_sb[:, :], bo_sb[:, :], gates[:, 2:3], None, ALU.mult))
            pool.wait_ge(xn_ready, NT)
            for t in range(NT):
                nc.gpsimd.tensor_tensor(x_sb[:, t, :], x_sb[:, t, :], bo_sb[:, :], ALU.add).then_inc(xb_done, 1)

            def prob_lo(j, g):
                if g == 0:
                    pool.wait_ge(ph_act, j + 1)
                else:
                    pool.wait_ge(ph_dve, j + 1)
                dst = slice(3 * g, 3 * g + 3)
                nc.gpsimd.tensor_tensor(p_lo[:, j % 3, dst, :].rearrange("p t n -> p (t n)"), prob[:, g, :],
                                        p_hi[:, j % 3, dst, :].rearrange("p t n -> p (t n)"),
                                        ALU.subtract).then_inc(pl_done, 1)

            for i in range(STEPS):
                if 0 <= i - HI_LAG < NH:
                    prob_lo(i - HI_LAG, 0)
                    prob_lo(i - HI_LAG, 1)
                for b, s in tail_of(i):
                    if s == TAIL_WO:
                        t = NT + QT * b
                        pool.wait_ge(var_ready, 2 + b)
                        nc.gpsimd.tensor_tensor(rstd[:, t:t + QT], vare[:, t:t + QT], c_mhalf[:, t:t + QT],
                                                ALU.pow).then_inc(rstd_ready, 1)
                    if s == TAIL_GATE:
                        pool.wait_ge(gexp_go, b + 1)
                        nc.gpsimd.tensor_tensor(gexp[:, QT * b:QT * b + QT, :], c_e[:, :, :],
                                                diff[:, QT * b:QT * b + QT, :], ALU.pow).then_inc(gexp_done, 1)
                k = i - FFN0 - 1
                if 0 <= k < NF:
                    pool.wait_ge(hh_done, k + 1)
                    nc.gpsimd.tensor_tensor(hid_lo[:, k % 2, :], hid[:, k % 2, :], hid_hi[:, k % 2, :],
                                            ALU.subtract).then_inc(hl_done, 1)

        @block.scalar
        def _(act):
            def split_a(w):
                act.wait_ge(ld_w[w], 16)
                nc.scalar.activation(wa[:, 0, w, :], ring_a(w), ACT.Copy, scale=S_W).then_inc(w_hi, 1)

            def tanh_gates():
                act.wait_ge(ld_small, 48)
                nc.scalar.activation(gates[:, 2:4], gates[:, 0:2], ACT.Tanh).then_inc(tanh_done, 1)

            for n, item in enumerate(ITEMS):
                for w in SPLIT_BEFORE.get(n, []):
                    split_a(w)
                if n == 8:
                    tanh_gates()
                act.wait_ge(item_ps, n + 1)
                src = item_out(n)
                kind = item[0]
                if kind == "tx":
                    dst, s = xT[:, 0, :], S_ACTV
                elif kind == "tc":
                    dst, s = cT[:, 0, item[1] * T2:(item[1] + 1) * T2], S_ACTV
                elif kind == "k":
                    _, b, p = item
                    if b > 0:
                        act.wait_ge(k_st[p], 96)
                    dst, s = k_nat[:, 0, p, :], 1.0 / S_W
                elif kind == "q":
                    dst, s = q_nat[:, 0, item[1], :], 1.0 / S_W
                else:
                    _, b, t = item
                    dst, s = v_hi[:, b * KT + t, :, 0:DH], 1.0 / S_W
                    src = src.rearrange("p (h d) -> p h d", d=DH)
                nc.scalar.activation(dst, src, ACT.Copy, scale=s).then_inc(item_hi, 1)

            def exp_half(j, g):
                act.wait_ge(score_ps, 2 * j + g + 1)
                if j >= 1:
                    act.wait_ge(pl_done, 2 * (j - 1) + g + 1)
                nc.scalar.activation(prob[:, g, :], span(2 + 2 * g, 3 * T1), ACT.Exp,
                                     scale=DH ** -0.5 / S_SCORE).then_inc(exp_done, 1)

            for i in range(STEPS):
                j = i - ST_LAG
                if 0 <= j < NH:
                    exp_half(j, 0)
                    act.wait_ge(exp_done, 2 * j + 1)
                    if j >= 3:
                        act.wait_ge(pv_ps, QT * (j - 2))
                    nc.scalar.activation(p_hi[:, j % 3, 0:3, :].rearrange("p t n -> p (t n)"), prob[:, 0, :],
                                         ACT.Copy).then_inc(ph_act, 1)
                    exp_half(j, 1)
                k = i - FFN0
                if 0 <= k < NF:
                    e = EORDER[k % NE]
                    if k >= 2:
                        act.wait_ge(hl_done, k - 1)
                    for c in range(HC):
                        act.wait_ge(h_ps, HC // 2 * k + c // 2 + 1)
                        nc.scalar.activation(hid[:, k % 2, c * T1:(c + 1) * T1],
                                             span(2 * (k % 2), HC * T1)[:, c * T1:(c + 1) * T1], ACT.Gelu,
                                             bias=b1T[:, e * HC + c:e * HC + c + 1],
                                             scale=1.0 / (S_ACTV * S_W)).then_inc(gelu_done, 1)
                j = i - FSPLIT0
                if 0 <= j < NE:
                    act.wait_ge(ld_f[j], 32)
                    nc.scalar.activation(wf[:, 0, EORDER[j], :, :], ring_f(j), ACT.Copy, scale=S_W).then_inc(f_hi, 1)
                for b, s in tail_of(i):
                    if s in (TAIL_O0, TAIL_O1):
                        act.wait_ge(misc_ps, MISC[(s, b)] + 1)
                        act_t = QT * b + s
                        nc.scalar.activation(oT[:, 0, act_t, :], misc, ACT.Copy, scale=S_ACTV).then_inc(misc_hi, 1)
                    if s == TAIL_X:
                        act.wait_ge(misc_ps, MISC[(s, b)] + 1)
                        nc.scalar.activation(x2h[:, 0, b * T1:(b + 1) * T1], misc[:, 0:T1], ACT.Copy,
                                             scale=S_ACTV).then_inc(misc_hi, 1)

        @block.vector
        def _(dve):
            n_chain = 0
            n_mhi = 0

            def link(ins):
                nonlocal n_chain
                n_chain += 1
                ins.then_inc(dve_chain, 1)
                dve.wait_ge(dve_chain, n_chain)

            def layernorm(src, first, tiles, phase):
                for t in range(tiles):
                    last = nc.vector.bn_stats(stats[:, first + t, :], src[:, t, :])
                    link(last)
                for t in range(tiles):
                    link(nc.vector.bn_aggr(mv[:, first + t, :], stats[:, first + t, :]))
                nc.vector.tensor_scalar(vare[:, first:first + tiles], mv[:, first:first + tiles, 1], EPS, None,
                                        ALU.add).then_inc(var_ready, 1)
                dve.wait_ge(rstd_ready, phase)
                for t in range(tiles):
                    nc.vector.tensor_scalar(xn[:, (first + t) % NT, :], src[:, t, :], mv[:, first + t, 0:1],
                                            rstd[:, first + t:first + t + 1], ALU.subtract,
                                            ALU.mult).then_inc(xn_ready, 1)

            def split_a(w):
                dve.wait_ge(w_hi, SPLIT_AT[w])
                nc.vector.scalar_tensor_tensor(out=wa[:, 1, w, :], in0=ring_a(w), scalar=S_W, in1=wa[:, 0, w, :],
                                               op0=ALU.mult, op1=ALU.subtract).then_inc(w_lo, 1)

            dve.wait_ge(ld_x, 16)
            layernorm(x_sb, 0, NT, 1)
            for n, item in enumerate(ITEMS):
                for w in SPLIT_BEFORE.get(n, []):
                    split_a(w)
                dve.wait_ge(item_hi, n + 1)
                src = item_out(n)
                kind = item[0]
                if kind == "tx":
                    dst, hi, s = xT[:, 1, :], xT[:, 0, :], S_ACTV
                elif kind == "tc":
                    cols = slice(item[1] * T2, (item[1] + 1) * T2)
                    dst, hi, s = cT[:, 1, cols], cT[:, 0, cols], S_ACTV
                elif kind == "k":
                    p = item[2]
                    dst, hi, s = k_nat[:, 1, p, :], k_nat[:, 0, p, :], 1.0 / S_W
                elif kind == "q":
                    p = item[1]
                    dst, hi, s = q_nat[:, 1, p, :], q_nat[:, 0, p, :], 1.0 / S_W
                else:
                    t = item[1] * KT + item[2]
                    dst, hi, s = v_lo[:, t, :, :], v_hi[:, t, :, 0:DH], 1.0 / S_W
                    src = src.rearrange("p (h d) -> p h d", d=DH)
                nc.vector.scalar_tensor_tensor(out=dst, in0=src, scalar=s, in1=hi, op0=ALU.mult,
                                               op1=ALU.subtract).then_inc(item_lo, 1)

            dve.wait_ge(tanh_done, 1)
            link(nc.vector.tensor_scalar(scales[:, 0:1], gates[:, 2:3], 1.0 / (S_ACTV * S_W), None, ALU.mult))
            link(nc.vector.tensor_scalar(scales[:, 1:2], gates[:, 3:4], 1.0 / S_W, None, ALU.mult))

            def take_max(i, q):
                dve.wait_ge(max_ps, QT * i + q + 1)
                nc.vector.tensor_reduce(nmax[:, i, q:q + 1], span(0, KEYS), AX_X, ALU.max,
                                        negate=True).then_inc(max_done, 1)

            def normalise(j):
                dve.wait_ge(pv_ps, QT * (j + 1))
                b, h = divmod(j, HEADS)
                link(nc.vector.reciprocal(rsum[:, j, :], o_ps[:, :, DH]))
                nc.vector.tensor_tensor(o_sb[:, QT * b:QT * b + QT, h * DH:(h + 1) * DH], o_ps[:, :, 0:DH],
                                        rsum[:, j, :].unsqueeze(2).broadcast_to([P, QT, DH]),
                                        ALU.mult).then_inc(o_done, 1)

            def lo_of_misc(dst, hi, n):
                nc.vector.scalar_tensor_tensor(out=dst, in0=misc[:, 0:n], scalar=S_ACTV, in1=hi, op0=ALU.mult,
                                               op1=ALU.subtract).then_inc(misc_done, 1)

            def tail(b, s):
                nonlocal n_mhi
                tiles = slice(QT * b, QT * b + QT)
                cols = slice(b * T1, (b + 1) * T1)
                dve.wait_ge(misc_ps, MISC[(s, b)] + 1)
                if s in (TAIL_O0, TAIL_O1, TAIL_X):
                    n_mhi += 1
                    dve.wait_ge(misc_hi, n_mhi)
                if s in (TAIL_O0, TAIL_O1):
                    t = QT * b + s
                    lo_of_misc(oT[:, 1, t, :], oT[:, 0, t, :], INNER)
                elif s == TAIL_WO:
                    dve.wait_ge(xb_done, NT)
                    nc.vector.scalar_tensor_tensor(
                        out=acc[:, tiles, :].rearrange("p t d -> p (t d)"), in0=misc[:, 0:QT * D],
                        scalar=scales[:, 0:1], in1=x_sb[:, tiles, :].rearrange("p t d -> p (t d)"),
                        op0=ALU.mult, op1=ALU.add).then_inc(misc_done, 1)
                    dve.wait_ge(misc_done, MISC[(s, b)] + 1)
                    layernorm(acc[:, tiles, :], NT + QT * b, QT, 2 + b)
                elif s == TAIL_X:
                    link(nc.vector.tensor_copy(x2T[:, cols], misc[:, 0:T1]))
                    lo_of_misc(x2h[:, 1, cols], x2h[:, 0, cols], T1)
                elif s == TAIL_GATE:
                    for t in range(QT):
                        ins = nc.vector.tensor_tensor(logit[:, QT * b + t, 0:E], misc[:, t * E:(t + 1) * E], gb[:, :],
                                                      ALU.add)
                        if t < QT - 1:
                            link(ins)
                    ins.then_inc(misc_done, 1)
                    dve.wait_ge(misc_done, MISC[(s, b)] + 1)
                    for t in range(QT * b, QT * b + QT):
                        link(nc.vector.max(top8[:, t, :], logit[:, t, 0:E]))
                        link(nc.vector.tensor_scalar(diff[:, t, :], logit[:, t, 0:E], top8[:, t, 0:1], None,
                                                     ALU.subtract))
                        link(nc.vector.tensor_copy(pick8[:, t, 0:2], top8[:, t, 0:2]))
                        link(nc.vector.match_replace(marked[:, t, :], pick8[:, t, :], logit[:, t, :], PICKED))
                    nc.vector.tensor_scalar(mask[:, tiles, :], marked[:, tiles, 0:E], PICKED, None,
                                            ALU.is_equal).then_inc(gexp_go, 1)
                    dve.wait_ge(gexp_go, b + 1)
                    dve.wait_ge(gexp_done, b + 1)
                    link(nc.vector.tensor_tensor(gexp[:, tiles, :], gexp[:, tiles, :], mask[:, tiles, :], ALU.mult))
                    link(nc.vector.tensor_reduce(gsum[:, tiles], gexp[:, tiles, :], AX_X, ALU.add))
                    link(nc.vector.reciprocal(grec[:, tiles], gsum[:, tiles]))
                    for t in range(QT * b, QT * b + QT):
                        link(nc.vector.tensor_scalar(comb[:, t, 0:E], gexp[:, t, :], grec[:, t:t + 1], None,
                                                     ALU.mult))
                    nc.vector.tensor_scalar(comb_s[:, tiles, :], comb[:, tiles, :], scales[:, 1:2], None,
                                            ALU.mult).then_inc(comb_ready, 1)
                    dve.wait_ge(comb_ready, b + 1)
                elif s == TAIL_COMB:
                    nc.vector.tensor_copy(combT[:, cols], misc[0:NE, 0:T1]).then_inc(misc_done, 1)
                elif s == TAIL_B2:
                    nc.vector.scalar_tensor_tensor(
                        out=acc[:, tiles, :].rearrange("p t d -> p (t d)"), in0=misc[:, 0:QT * D],
                        scalar=gates[:, 3:4], in1=acc[:, tiles, :].rearrange("p t d -> p (t d)"),
                        op0=ALU.mult, op1=ALU.add).then_inc(misc_done, 1)
                    dve.wait_ge(misc_done, MISC[(s, b)] + 1)

            for i in range(STEPS):
                if 0 <= i - NORM_LAG < NH:
                    normalise(i - NORM_LAG)
                if 1 <= i <= NH:
                    dve.wait_ge(misc_ps, MISC[("shift", i - 1)] + 1)
                    b, h = divmod(i - 1, HEADS)
                    nc.vector.tensor_copy(q_b[DH:DH + 1, h, b * T1:(b + 1) * T1],
                                          misc[DH:DH + 1, 0:T1]).then_inc(misc_done, 1)
                if i < NH:
                    take_max(i, 0)
                if 0 <= i - HI_LAG < NH:
                    j = i - HI_LAG
                    dve.wait_ge(exp_done, 2 * j + 2)
                    if j >= 3:
                        dve.wait_ge(pv_ps, QT * (j - 2))
                    nc.vector.tensor_copy(p_hi[:, j % 3, 3:6, :].rearrange("p t n -> p (t n)"),
                                          prob[:, 1, :]).then_inc(ph_dve, 1)
                if i < NH:
                    take_max(i, 1)
                    dve.wait_ge(max_done, QT * (i + 1))
                    nc.vector.tensor_scalar(shift16[:, i, :], nmax[:, i, :], 1.0 / SHIFT_ROW, SHIFT_P, ALU.mult,
                                            ALU.add).then_inc(shift_ready, 1)
                k = i - FFN0 - 1
                if 0 <= k < NF:
                    dve.wait_ge(gelu_done, HC * (k + 1))
                    if k >= 2:
                        dve.wait_ge(y_ps, k - 1)
                    nc.vector.tensor_copy(hid_hi[:, k % 2, :], hid[:, k % 2, :]).then_inc(hh_done, 1)
                k = i - FFN0 - 3
                if 0 <= k < NF:
                    b, e = k // NE, EORDER[k % NE]
                    dve.wait_ge(y_ps, k + 1)
                    for t in range(QT):
                        ins = nc.vector.scalar_tensor_tensor(
                            out=acc[:, QT * b + t, :], in0=banks[:, 4 + k % 2, t * D:(t + 1) * D],
                            scalar=comb_s[:, QT * b + t, e:e + 1], in1=acc[:, QT * b + t, :],
                            op0=ALU.mult, op1=ALU.add)
                        if t < QT - 1:
                            link(ins)
                    ins.then_inc(y_done, 1)
                    dve.wait_ge(y_done, k + 1)
                j = i - FSPLIT0
                if 0 <= j < NE:
                    dve.wait_ge(f_hi, j + 1)
                    e = EORDER[j]
                    nc.vector.scalar_tensor_tensor(
                        out=wf[:, 1, e, :, :].rearrange("p a n -> p (a n)"),
                        in0=ring_f(j).rearrange("p a n -> p (a n)"), scalar=S_W,
                        in1=wf[:, 0, e, :, :].rearrange("p a n -> p (a n)"),
                        op0=ALU.mult, op1=ALU.subtract).then_inc(f_lo, 1)
                if i == BIAS_STEP:
                    dve.wait_ge(misc_ps, MISC[("b1", 0)] + 1)
                    nc.vector.tensor_copy(b1T[:, :], misc[:, 0:NE * HC]).then_inc(misc_done, 1)
                for b, s in tail_of(i):
                    tail(b, s)

        @block.tensor
        def _(pe):
            def three(dst, w, a, start=True, stop=True):
                nc.tensor.matmul(dst, w[0], a[0], start=start, stop=False)
                nc.tensor.matmul(dst, w[0], a[1], start=False, stop=False)
                return nc.tensor.matmul(dst, w[1], a[0], start=False, stop=stop)

            def w_pair(w, cols):
                return wa[:, 0, w, cols], wa[:, 1, w, cols]

            def x_pair(cols):
                return xT[:, 0, cols], xT[:, 1, cols]

            def c_pair(cols):
                return cT[:, 0, cols], cT[:, 1, cols]

            pe.wait_ge(consts, 3)
            for n, item in enumerate(ITEMS):
                kind = item[0]
                dst = item_out(n)
                if n >= 4:
                    pe.wait_ge(item_lo, n - 3)
                if kind == "tx":
                    for t in range(NT):
                        pe.wait_ge(xn_ready, t + 1)
                        last = nc.tensor.transpose(dst[:, t * P:(t + 1) * P], xn[:, t, :], ident[:, :])
                elif kind == "tc":
                    b = item[1]
                    pe.wait_ge(ld_ctx[b], 16)
                    for t in range(T2 // P):
                        last = nc.tensor.transpose(dst[:, t * P:(t + 1) * P], ctx_sb[:, b * (T2 // P) + t, :],
                                                   ident[:, :])
                elif kind == "k":
                    _, b, p = item
                    pair = slice(p * P, (p + 1) * P)
                    pe.wait_ge(w_lo, SPLIT_AT[WK1])
                    pe.wait_ge(item_lo, ITEMS.index(("tc", b)) + 1)
                    three(dst[:, 0:T2], w_pair(WK2, pair), c_pair(slice(b * T2, (b + 1) * T2)))
                    last = three(dst[:, T2:KEYS], w_pair(WK1, pair), x_pair(slice(b * T1, (b + 1) * T1)))
                elif kind == "q":
                    p = item[1]
                    pe.wait_ge(w_lo, SPLIT_AT[WQ])
                    last = three(dst, w_pair(WQ, slice(p * P, (p + 1) * P)), x_pair(slice(0, B * T1)))
                else:
                    _, b, t = item
                    if t < T2 // P:
                        pe.wait_ge(w_lo, SPLIT_AT[WV2])
                        pe.wait_ge(item_lo, ITEMS.index(("tc", b)) + 1)
                        last = three(dst, c_pair(ctx_cols(b, t)), w_pair(WV2, slice(0, INNER)))
                    else:
                        pe.wait_ge(w_lo, SPLIT_AT[WV1])
                        at = b * T1 + (t - T2 // P) * P
                        last = three(dst, x_pair(slice(at, at + P)), w_pair(WV1, slice(0, INNER)))
                last.then_inc(item_ps, 1)

            def max_scores(i, q):
                b, h = divmod(i, HEADS)
                if q == 0:
                    pe.wait_ge(k_st[b * PAIRS + h // 2], 96)
                    pe.wait_ge(q_st[h // 2], 96)
                if i + q > 0:
                    pe.wait_ge(max_done, QT * i + q)
                queries = q_a[0:DH, h, b * T1 + q * P:b * T1 + (q + 1) * P]
                nc.tensor.matmul(span(0, KEYS)[:, 0:T2], queries, k_a[0:DH, h, 0:T2], start=True, stop=True)
                nc.tensor.matmul(span(0, KEYS)[:, T2:KEYS], queries, k_a[0:DH, h, T2:KEYS], start=True,
                                 stop=True).then_inc(max_ps, 1)

            def scores(j, g):
                b, h = divmod(j, HEADS)
                if g == 0:
                    pe.wait_ge(misc_done, MISC[("shift", j)] + 1)
                if j >= 1:
                    pe.wait_ge(exp_done, 2 * (j - 1) + g + 1)
                dst = span(2 + 2 * g, 3 * T1)
                queries = slice(b * T1, (b + 1) * T1)
                for n in range(3):
                    t = 3 * g + n
                    keys = slice(t * P, (t + 1) * P)
                    cols = slice(n * T1, (n + 1) * T1)
                    nc.tensor.matmul(dst[:, cols], k_a[:, h, keys], q_a[:, h, queries], start=True, stop=False)
                    last = nc.tensor.matmul(dst[:, cols], k_b[0:DH + 1, h, keys], q_b[0:DH + 1, h, queries],
                                            start=False, stop=True)
                last.then_inc(score_ps, 1)

            def shift_row(i):
                pe.wait_ge(shift_ready, i + 1)
                if MISC[("shift", i)] > 0:
                    pe.wait_ge(misc_done, MISC[("shift", i)])
                for q in range(QT):
                    last = nc.tensor.matmul(misc[DH:DH + 1, q * P:(q + 1) * P], shift16[:, i, q:q + 1],
                                            ident16[:, :], start=True, stop=True)
                last.then_inc(misc_ps, 1)

            def values(j, q):
                b, h = divmod(j, HEADS)
                if q == 0:
                    pe.wait_ge(pl_done, 2 * (j + 1))
                    if j >= 1:
                        pe.wait_ge(o_done, j)
                cols = slice(q * P, (q + 1) * P)
                for t in range(KT):
                    vh, vl = v_hi[:, b * KT + t, h, :], v_lo[:, b * KT + t, h, :]
                    ph, pl = p_hi[:, j % 3, t, cols], p_lo[:, j % 3, t, cols]
                    nc.tensor.matmul(o_ps[:, q, :], ph, vh, start=(t == 0), stop=False, skip_group_check=True)
                    nc.tensor.matmul(o_ps[:, q, 0:DH], ph, vl, start=False, stop=False, skip_group_check=True)
                    last = nc.tensor.matmul(o_ps[:, q, :], pl, vh, start=False, stop=(t == KT - 1),
                                            skip_group_check=True)
                last.then_inc(pv_ps, 1)

            def tail(b, s):
                pe.wait_ge(misc_done, MISC[(s, b)])
                if s in (TAIL_O0, TAIL_O1):
                    pe.wait_ge(o_done, HEADS * (b + 1))
                    for c in range(INNER // P):
                        last = nc.tensor.transpose(misc[:, c * P:(c + 1) * P],
                                                   o_sb[:, QT * b + s, c * P:(c + 1) * P], ident[:, :])
                elif s == TAIL_WO:
                    for q in range(QT):
                        t = QT * b + q
                        for c in range(INNER // P):
                            cols = slice(c * P, (c + 1) * P)
                            last = three(misc[:, q * D:(q + 1) * D], (oT[:, 0, t, cols], oT[:, 1, t, cols]),
                                         w_pair(WO, cols), start=(c == 0), stop=(c == INNER // P - 1))
                elif s == TAIL_X:
                    pe.wait_ge(xn_ready, NT + QT * (b + 1))
                    for q in range(QT):
                        last = nc.tensor.transpose(misc[:, q * P:(q + 1) * P], xn[:, QT * b + q, :], ident[:, :])
                elif s == TAIL_GATE:
                    pe.wait_ge(ld_rows, 96)
                    for q in range(QT):
                        at = b * T1 + q * P
                        last = nc.tensor.matmul(misc[:, q * E:(q + 1) * E], x2T[:, at:at + P], gw[:, :],
                                                start=True, stop=True)
                elif s == TAIL_COMB:
                    pe.wait_ge(comb_ready, b + 1)
                    for q in range(QT):
                        last = nc.tensor.transpose(misc[0:NE, q * P:(q + 1) * P], comb[:, QT * b + q, :],
                                                   ident[:, :])
                else:
                    for q in range(QT):
                        at = b * T1 + q * P
                        last = nc.tensor.matmul(misc[:, q * D:(q + 1) * D], combT[:, at:at + P], b2_rows[:, :],
                                                start=True, stop=True)
                last.then_inc(misc_ps, 1)

            for i in range(STEPS):
                k = i - FFN0
                if 0 <= k < NF:
                    b, e = k // NE, EORDER[k % NE]
                    if k == 0:
                        pe.wait_ge(max_done, QT * NH)
                    if k == 1:
                        pe.wait_ge(exp_done, 2 * NH)
                    if k >= 2:
                        pe.wait_ge(gelu_done, HC * (k - 1))
                    if k < NE:
                        pe.wait_ge(f_lo, k + 1)
                    if k % NE == 0:
                        pe.wait_ge(misc_done, MISC[(TAIL_X, b)] + 1)
                    tok = slice(b * T1, (b + 1) * T1)
                    for c in range(HC):
                        cols = slice(c * P, (c + 1) * P)
                        last = three(span(2 * (k % 2), HC * T1)[:, c * T1:(c + 1) * T1],
                                     (wf[:, 0, e, 0, cols], wf[:, 1, e, 0, cols]),
                                     (x2h[:, 0, tok], x2h[:, 1, tok]))
                        if c % 2 == 1:
                            last.then_inc(h_ps, 1)
                if i < NH:
                    if i == 0:
                        pe.wait_ge(item_lo, NI)
                        pe.wait_ge(consts, 8)
                    max_scores(i, 0)
                if 0 <= i - PV_LAG < NH:
                    values(i - PV_LAG, 0)
                if 1 <= i <= NH:
                    shift_row(i - 1)
                if 0 <= i - ST_LAG < NH:
                    scores(i - ST_LAG, 0)
                if i < NH:
                    max_scores(i, 1)
                if 0 <= i - ST_LAG < NH:
                    scores(i - ST_LAG, 1)
                if 0 <= i - PV_LAG < NH:
                    values(i - PV_LAG, 1)
                k = i - FFN0 - 2
                if 0 <= k < NF:
                    e = EORDER[k % NE]
                    pe.wait_ge(hl_done, k + 1)
                    if k >= 2:
                        pe.wait_ge(y_done, k - 1)
                    for q in range(QT):
                        for c in range(HC):
                            at = c * T1 + q * P
                            cols = slice(c * P, (c + 1) * P)
                            last = three(banks[:, 4 + k % 2, q * D:(q + 1) * D],
                                         (hid_hi[:, k % 2, at:at + P], hid_lo[:, k % 2, at:at + P]),
                                         (wf[:, 0, e, 1, cols], wf[:, 1, e, 1, cols]),
                                         start=(c == 0), stop=(c == HC - 1))
                    last.then_inc(y_ps, 1)
                if i == BIAS_STEP:
                    pe.wait_ge(ld_rows, 96)
                    pe.wait_ge(misc_done, MISC[("b1", 0)])
                    nc.tensor.transpose(misc[:, 0:NE * HC], b1_rows[:, :],
                                        ident[0:NE * HC, 0:NE * HC]).then_inc(misc_ps, 1)
                for b, s in tail_of(i):
                    tail(b, s)


_INS = ['x', 'ctx_1024', 'g_xattn', 'g_ffn', 'L0_xattn_Wq1', 'L0_xattn_Wk1', 'L0_xattn_Wv1', 'L0_xattn_Wk2',
        'L0_xattn_Wv2', 'L0_xattn_Wo', 'L0_xattn_bo', 'L0_ffn_gate_w', 'L0_ffn_gate_b', 'L0_ffn_w1', 'L0_ffn_b1',
        'L0_ffn_w2', 'L0_ffn_b2', 'L0_ffn_ws1', 'L0_ffn_bs1', 'L0_ffn_ws2', 'L0_ffn_bs2']
_OUTS = [((B, T1, D), 'float32')]


def kernel(**inputs):
    import numpy as _np
    import concourse.bacc as _bacc
    from concourse import mybir as _mybir
    from concourse.bass_utils import run_bass_kernel_spmd as _run

    nc = _bacc.Bacc("TRN2", target_bir_lowering=False, num_devices=1)
    arrays, args = {}, []
    for name in _INS:
        a = _np.ascontiguousarray(inputs[name])
        arrays[f"in_{name}_dram"] = a
        args.append(nc.dram_tensor(f"in_{name}_dram", a.shape, _mybir.dt.from_np(a.dtype), kind="ExternalInput").ap())
    for i, (shape, dtype) in enumerate(_OUTS):
        dt = _mybir.dt.from_np(_np.dtype(dtype))
        args.append(nc.dram_tensor(f"out_{i}_dram", shape, dt, kind="ExternalOutput").ap())
    block_kernel(nc, *args)
    r = _run(nc, [arrays], core_ids=[0])
    got = tuple(r.results[0][f"out_{i}_dram"] for i in range(len(_OUTS)))
    return got[0]
```

```python
from contextlib import ExitStack
from math import log

import concourse.bass as bass
from concourse import mybir

F32 = mybir.dt.float32
F16 = mybir.dt.float16
ALU = mybir.AluOpType
ACT = mybir.ActivationFunctionType
AX_X = mybir.AxisListType.X

P = 128
B = 2
T1 = 256
T2 = 512
D = 128
HEADS = 8
DH = 64
INNER = HEADS * DH
PAIRS = HEADS // 2
KEYS = T1 + T2
KT = KEYS // P
QT = T1 // P
NT = B * QT
NH = B * HEADS
E = 8
NE = E + 1
HID = 512
HC = HID // P
NW = 6
WK2, WK1, WQ, WV2, WV1, WO = range(NW)
RING = 4
EORDER = [E] + list(range(E))
EPS = 1e-5

S_ACTV = 64.0
S_W = 1024.0
S_SCORE = S_ACTV * S_ACTV
SHIFT_ROW = S_SCORE
P_SCALE = S_ACTV
SHIFT_P = log(P_SCALE) * DH ** 0.5
NONE = -3.0e38
PICKED = 3.0e38

ST_LAG = 2
HI_LAG = 3
PV_LAG = 4
NORM_LAG = 5
FFN0 = NH + ST_LAG
NF = B * NE
STEPS = FFN0 + NF + 4
TAIL0 = [HEADS - 1 + NORM_LAG, NH + NORM_LAG]
BIAS_STEP = 10
EARLY = 3
FSPLIT0 = 15
TAIL_O0, TAIL_O1, TAIL_WO, TAIL_X, TAIL_GATE, TAIL_COMB, TAIL_B2 = TAIL_STAGES = (0, 1, 2, 4, 5, 7, 8)


def late_items(i, q):
    n = NI - LATE + LATE // 4 * (2 * i + q)
    return range(n, n + LATE // 4) if i < 2 else []


def place(h):
    return h % 2 * PAIRS + h // 2


def tail_of(i):
    return [(b, i - TAIL0[b]) for b in range(B) if i - TAIL0[b] in TAIL_STAGES]


def plan_items():
    items = [("tc", 0), ("tx", 0)]
    for p in range(PAIRS):
        items += [("k", 0, p), ("q", p)]
    items += [("v", 0, 0), ("tc", 1)]
    items += [("v", 0, t) for t in range(1, KT)]
    items += [("v", 1, t) for t in range(KT)]
    items += [("k", 1, p) for p in range(PAIRS)]
    return items


ITEMS = plan_items()
NI = len(ITEMS)
LATE = 8
SLOT = [n % 4 for n in range(NI - LATE)] + [1 + n % 2 for n in range(LATE)]


def before(n, slot):
    return max([m + 1 for m in range(n) if SLOT[m] == slot], default=0)


SPLIT_BEFORE = {1: [WK2, WK1], 2: [WQ], 5: [WV2], 8: [WV1], 10: [WO]}
SPLIT_ORDER = [w for n in sorted(SPLIT_BEFORE) for w in SPLIT_BEFORE[n]]
SPLIT_AT = {w: SPLIT_ORDER.index(w) + 1 for w in SPLIT_ORDER}


GROUPS = [[(0, 1), (1, PAIRS)], [(0, 2), (2, PAIRS)]]


def group_of(b, p):
    return max(p0 for p0, _ in GROUPS[b] if p0 <= p)


LO_LAST = NH - 3


def lo_tiles(j):
    return 2 if j < LO_LAST else 0


def pool_lo(j, g):
    return 2 * j + g + 1 - max(0, j - LO_LAST + (g == 1)) if j >= 0 else 0


def shifts_before(n):
    return sum(1 for u, m in MISC.items() if m < n and u[0] == "shift")


def plan_misc():
    uses = []
    for i in range(STEPS):
        if 1 <= i <= NH:
            uses.append(("shift", i - 1))
        if i == BIAS_STEP:
            uses.append(("b1", 0))
        for b, s in tail_of(i):
            uses.append((s, b))
    return {u: n for n, u in enumerate(uses)}


MISC = plan_misc()


def block_kernel(nc, x, ctx_in, g_xattn, g_ffn, Wq1, Wk1, Wv1, Wk2, Wv2, Wo, bo,
                 gate_w, gate_b, w1, b1, w2, b2, ws1, bs1, ws2, bs2, out):
    stack = ExitStack()
    with stack:
        def sb(name, shape, dt):
            return stack.enter_context(nc.sbuf_tensor(name, shape, dt))

        def sem(name):
            return stack.enter_context(nc.semaphore(name))

        x_sb = sb("x_sb", [P, NT, D], F32)
        early = sb("early", [P, 4 * (KEYS // 2) * QT], F32)
        ctx_sb = early[:, 0:B * T2 // P * D].rearrange("p (t d) -> p t d", d=D)
        prob = early[:, :].rearrange("p (a g n) -> p a g n", a=2, g=2)
        xT = sb("xT", [P, 2, B * T1], F16)
        cT = sb("cT", [P, 2, B * T2], F16)
        ring = sb("ring", [P, RING, 2, 512], F32)
        wa = sb("wa", [P, 2, NW, 512], F16)
        wf = sb("wf", [P, 2, NE, 2, 512], F16)
        kab = sb("kab", [P, 2, HEADS, KEYS], F16)
        k_a = kab[:, 0]
        k_b = kab[:, 1]
        kflat = kab[:, :, :, :].rearrange("p a h n -> p (a h n)")
        hid = kflat[:, 0:4096].bitcast(F32).rearrange("p (u n) -> p u n", u=2)
        hid_hi = kflat[:, 4096:6144].rearrange("p (u n) -> p u n", u=2)
        hid_lo = kflat[:, 6144:8192].rearrange("p (u n) -> p u n", u=2)
        k_nat = sb("k_nat", [P, 2, PAIRS, KEYS], F16)
        qab = sb("qab", [P, 2, HEADS, B * T1], F16)
        q_a = qab[:, 0]
        q_b = qab[:, 1]
        qo = sb("qo", [P, 2, 4, 512], F16)
        q_nat = qo
        oT = qo
        v_hi = sb("v_hi", [P, B * KT, HEADS, DH + 1], F16)
        v_lo = sb("v_lo", [P, B * KT, HEADS, DH], F16)
        p_hi = sb("p_hi", [P, 3, KT, T1], F16)
        p_lo = sb("p_lo", [P, 3, KT, T1], F16)
        o_sb = sb("o_sb", [P, NT, INNER], F32)
        xn = sb("xn", [P, NT, D], F32)
        acc = sb("acc", [P, NT, D], F32)
        x2T = sb("x2T", [P, NT * P], F32)
        x2h = sb("x2h", [P, 2, NT * P], F16)
        ident = sb("ident", [P, P], F32)
        ident16 = sb("ident16", [P, P], F16)
        b1_rows = sb("b1_rows", [NE * HC, P], F32)
        b1T = sb("b1T", [P, NE * HC], F32)
        b2_rows = sb("b2_rows", [NE, D], F32)
        gw = sb("gw", [P, E], F32)
        gb = sb("gb", [P, E], F32)
        bo_sb = sb("bo_sb", [P, D], F32)
        gates = sb("gates", [P, 4], F32)
        scales = sb("scales", [P, 2], F32)
        nmax = sb("nmax", [P, NH, QT], F32)
        shift16 = sb("shift16", [P, NH, QT], F16)
        rsum = sb("rsum", [P, NH, QT], F32)
        stats = sb("stats", [P, 2 * NT, 6], F32)
        mv = sb("mv", [P, 2 * NT, 2], F32)
        vare = sb("vare", [P, 2 * NT], F32)
        rstd = sb("rstd", [P, 2 * NT], F32)
        c_mhalf = sb("c_mhalf", [P, 2 * NT], F32)
        c_sw = sb("c_sw", [P, 1], F32)
        c_e = sb("c_e", [P, QT], F32)
        logit = sb("logit", [P, NT, 2 * E], F32)
        top8 = sb("top8", [P, NT, 8], F32)
        pick8 = sb("pick8", [P, NT, 8], F32)
        marked = sb("marked", [P, NT, 2 * E], F32)
        mask = sb("mask", [P, NT, E], F32)
        first = sb("first", [P, NT, E], F32)
        gdiff = sb("gdiff", [P, NT], F32)
        gexp = sb("gexp", [P, NT], F32)
        gsum = sb("gsum", [P, NT], F32)
        gtop = sb("gtop", [P, NT, 2], F32)
        comb = sb("comb", [P, NT, NE], F32)
        comb_s = sb("comb_s", [P, NT, NE], F32)
        combT = cT[0:NE, 0, :].bitcast(F32)

        banks = stack.enter_context(nc.psum_tensor("banks", [P, 8, 512], F32))

        def span(first, n):
            return banks[:, first:first + 2, :].rearrange("p a n -> p (a n)")[:, 0:n]

        o_ps = banks[:, 6, 0:QT * (DH + 1)].rearrange("p (q d) -> p q d", q=QT)
        misc = banks[:, 7, :]

        ld_x, ld_small, ld_rows = sem("ld_x"), sem("ld_small"), sem("ld_rows")
        ld_ctx = [sem(f"ld_ctx{b}") for b in range(B)]
        ld_w = [sem(f"ld_w{w}") for w in range(NW)]
        ld_f = [sem(f"ld_f{j}") for j in range(NE)]
        consts = sem("consts")
        pool_chain = sem("pool_chain")
        dve_chain = sem("dve_chain")
        var_ready = sem("var_ready")
        rstd_ready = sem("rstd_ready")
        xn_ready = sem("xn_ready")
        tanh_done = sem("tanh_done")
        xb_done = sem("xb_done")
        w_hi, w_lo = sem("w_hi"), sem("w_lo")
        item_ps = sem("item_ps")
        item_hi, item_lo = sem("item_hi"), sem("item_lo")
        k_st = [sem(f"k_st{n}") for n in range(B * PAIRS)]
        q_st = [sem(f"q_st{n}") for n in range(PAIRS)]
        max_ps = sem("max_ps")
        max_done = sem("max_done")
        shift_ready = sem("shift_ready")
        shift_done = sem("shift_done")
        score_ps = sem("score_ps")
        exp_done = sem("exp_done")
        ph_act, ph_dve = sem("ph_act"), sem("ph_dve")
        pl_done = sem("pl_done")
        pd_done = sem("pd_done")
        pv_ps = sem("pv_ps")
        o_done = sem("o_done")
        misc_ps = sem("misc_ps")
        misc_hi = sem("misc_hi")
        misc_done = sem("misc_done")
        gexp_go, gexp_done = sem("gexp_go"), sem("gexp_done")
        comb_ready = sem("comb_ready")
        e_scaled, e_hi, e_lo = sem("e_scaled"), sem("e_hi"), sem("e_lo")
        f_hi, f_lo = sem("f_hi"), sem("f_lo")
        h_ps = sem("h_ps")
        gelu_done = sem("gelu_done")
        hh_done, hl_done = sem("hh_done"), sem("hl_done")
        y_ps = sem("y_ps")
        y_done = sem("y_done")
        stored = sem("stored")

        x_d = x.rearrange("b (t p) d -> p (b t) d", p=P)
        ctx_d = ctx_in.rearrange("b (t p) d -> b p t d", p=P)
        out_d = out.rearrange("b (t p) d -> b p t d", p=P)
        w_d = {WK2: Wk2, WK1: Wk1, WQ: Wq1, WV2: Wv2, WV1: Wv1}

        def ring_a(w):
            n = SPLIT_AT[w] - 1
            return ring[:, n // 2, n % 2, :]

        def ring_f(j):
            return ring[:, (3 + j) % RING]

        def ctx_cols(b, t):
            return slice(b * T2 + t * P, b * T2 + (t + 1) * P)

        def item_out(n):
            kind = ITEMS[n][0]
            return span(2 * SLOT[n], KEYS if kind == "k" else 512)

        block = stack.enter_context(nc.Block())

        @block.sync
        def _(sp):
            def load_a(w):
                dst = ring_a(w)
                if w == WO:
                    sp.dma_start(dst.rearrange("p (c n) -> p c n", n=D),
                                 Wo.rearrange("(c p) n -> p c n", p=P)).then_inc(ld_w[w], 16)
                else:
                    sp.dma_start(dst, w_d[w]).then_inc(ld_w[w], 16)

            def load_f(j):
                e = EORDER[j]
                slot = ring_f(j)
                src1, src2 = (ws1, ws2) if e == E else (w1[e], w2[e])
                if 1 <= j < RING:
                    sp.wait_ge(w_lo, 2 * j)
                elif RING <= j < RING + EARLY:
                    sp.wait_ge(e_lo, j - RING + 1)
                elif j >= RING + EARLY:
                    sp.wait_ge(f_lo, j - RING - EARLY + 1)
                sp.dma_start(slot[:, 0, :], src1).then_inc(ld_f[j], 16)
                sp.dma_start(slot[:, 1, :].rearrange("p (c n) -> p c n", n=D),
                             src2.rearrange("(c p) n -> p c n", p=P)).then_inc(ld_f[j], 16)

            sp.dma_start(x_sb[:, :, :], x_d).then_inc(ld_x, 16)
            sp.dma_start(ctx_sb[:, 0:T2 // P, :], ctx_d[0]).then_inc(ld_ctx[0], 16)
            for w in (WK2, WK1, WQ):
                load_a(w)
            sp.dma_start(gates[:, 0:1], g_xattn.partition_broadcast(P)).then_inc(ld_small, 16)
            sp.dma_start(gates[:, 1:2], g_ffn.partition_broadcast(P)).then_inc(ld_small, 16)
            sp.dma_start(ctx_sb[:, T2 // P:, :], ctx_d[1]).then_inc(ld_ctx[1], 16)
            for w in (WV2, WV1, WO):
                load_a(w)
            sp.dma_start(bo_sb[:, :], bo.partition_broadcast(P)).then_inc(ld_small, 16)
            sp.dma_start(gb[:, :], gate_b.partition_broadcast(P)).then_inc(ld_rows, 16)
            sp.dma_start(gw[:, :], gate_w).then_inc(ld_rows, 16)
            sp.dma_start(b1_rows[0:E * HC, :], b1.rearrange("e (c p) -> (e c) p", p=P)).then_inc(ld_rows, 16)
            sp.dma_start(b1_rows[E * HC:, :], bs1.rearrange("(c p) -> c p", p=P)).then_inc(ld_rows, 16)
            sp.dma_start(b2_rows[0:E, :], b2).then_inc(ld_rows, 16)
            sp.dma_start(b2_rows[E:, :], bs2.rearrange("(a n) -> a n", a=1)).then_inc(ld_rows, 16)

            def stack_k(b, p0, p1):
                done = k_st[b * PAIRS + p0]
                n = p1 - p0
                sp.wait_ge(item_lo, ITEMS.index(("k", b, p1 - 1)) + 1)
                if b > 0:
                    sp.wait_ge(score_ps, 2 * 2 * p1)
                for half in range(2):
                    src = slice(DH * half, DH * half + DH)
                    heads = slice(place(2 * p0 + half), place(2 * p1 + half - 2) + 1)
                    sp.dma_start(kab[0:DH, :, heads, :],
                                 k_nat[src, 0:1, p0:p1, :].broadcast_to([DH, 2, p1 - p0, KEYS])).then_inc(done, 16)
                    sp.dma_start(kab[DH:P, 0, heads, :], k_nat[src, 1, p0:p1, :]).then_inc(done, 16)

            def stack_q(p0, p1):
                done = q_st[p0]
                sp.wait_ge(item_lo, ITEMS.index(("q", p1 - 1)) + 1)
                for half in range(2):
                    src = slice(DH * half, DH * half + DH)
                    heads = slice(place(2 * p0 + half), place(2 * p1 + half - 2) + 1)
                    sp.dma_start(qab[0:DH, :, heads, :], q_nat[src, :, p0:p1, :]).then_inc(done, 16)
                    sp.dma_start(qab[DH:P, 0, heads, :], q_nat[src, 0, p0:p1, :]).then_inc(done, 16)

            load_f(0)
            for n, (p0, p1) in enumerate(GROUPS[0]):
                stack_k(0, p0, p1)
                stack_q(p0, p1)
                load_f(1 + n)
            for j in range(1 + len(GROUPS[0]), RING):
                load_f(j)
            for p0, p1 in GROUPS[1]:
                stack_k(1, p0, p1)
            for j in range(RING, NE):
                load_f(j)
            for b in range(B):
                sp.wait_ge(y_done, NE * (b + 1))
                sp.dma_start(out_d[b], acc[:, QT * b:QT * b + QT, :]).then_inc(stored, 16)
            sp.wait_ge(stored, 16 * B)

        @block.gpsimd
        def _(pool):
            n = 0

            def link(ins):
                nonlocal n
                n += 1
                ins.then_inc(pool_chain, 1)
                pool.wait_ge(pool_chain, n)

            nc.gpsimd.memset(c_mhalf[:, :], -0.5).then_inc(consts, 1)
            link(nc.gpsimd.memset(ident[:, :], 0.0))
            nc.gpsimd.affine_select(out=ident[:, :], in_=ident[:, :], compare_op=ALU.not_equal, fill=1.0,
                                    base=0, pattern=[[-1, P]], channel_multiplier=1).then_inc(consts, 1)
            link(nc.gpsimd.memset(ident16[:, :], 0.0))
            nc.gpsimd.affine_select(out=ident16[:, :], in_=ident16[:, :], compare_op=ALU.not_equal, fill=1.0,
                                    base=0, pattern=[[-1, P]], channel_multiplier=1).then_inc(consts, 1)
            pool.wait_ge(consts, 1)
            pool.wait_ge(var_ready, 1)
            nc.gpsimd.tensor_tensor(rstd[:, 0:NT], vare[:, 0:NT], c_mhalf[:, 0:NT], ALU.pow).then_inc(rstd_ready, 1)
            pool.wait_ge(rstd_ready, 1)
            nc.gpsimd.memset(k_b[DH:DH + 1, :, :], SHIFT_ROW).then_inc(consts, 1)
            pool.wait_ge(consts, 4)
            nc.gpsimd.memset(v_hi[:, :, :, DH:DH + 1], S_ACTV).then_inc(consts, 1)
            nc.gpsimd.memset(c_sw[:, :], S_W).then_inc(pool_chain, 1)
            n += 1
            link(nc.gpsimd.memset(c_e[:, :], 2.718281828459045))
            nc.gpsimd.memset(logit[:, :, :], NONE).then_inc(consts, 1)
            nc.gpsimd.memset(pick8[:, :, :], NONE).then_inc(consts, 1)
            nc.gpsimd.memset(comb[:, :, :], 1.0).then_inc(consts, 1)

            def split_early(j):
                pool.wait_ge(ld_f[j], 32)
                src = ring_f(j).rearrange("p a n -> p (a n)")
                hi = wf[:, 0, EORDER[j], :, :].rearrange("p a n -> p (a n)")
                power = c_sw[:, :].broadcast_to([P, 2 * 512])
                nc.gpsimd.tensor_tensor(hi, src, power, ALU.mult).then_inc(e_hi, 1)
                pool.wait_ge(e_hi, j + 1)
                nc.gpsimd.tensor_tensor(src, src, power, ALU.mult).then_inc(e_scaled, 1)
                pool.wait_ge(e_scaled, j + 1)
                nc.gpsimd.tensor_tensor(wf[:, 1, EORDER[j], :, :].rearrange("p a n -> p (a n)"), src, hi,
                                        ALU.subtract).then_inc(e_lo, 1)

            split_early(0)
            pool.wait_ge(tanh_done, 1)
            pool.wait_ge(ld_small, 48)
            link(nc.gpsimd.tensor_scalar(bo_sb[:, :], bo_sb[:, :], gates[:, 2:3], None, ALU.mult))
            pool.wait_ge(xn_ready, NT)
            for t in range(NT):
                nc.gpsimd.tensor_tensor(x_sb[:, t, :], x_sb[:, t, :], bo_sb[:, :], ALU.add).then_inc(xb_done, 1)

            def prob_lo(j, g):
                if g == 0:
                    pool.wait_ge(ph_act, j + 1)
                else:
                    pool.wait_ge(ph_dve, j + 1)
                n = lo_tiles(j) if g else 3
                dst = slice(3 * g, 3 * g + n)
                nc.gpsimd.tensor_tensor(p_lo[:, j % 3, dst, :].rearrange("p t n -> p (t n)"),
                                        prob[:, j % 2, g, 0:n * T1],
                                        p_hi[:, j % 3, dst, :].rearrange("p t n -> p (t n)"),
                                        ALU.subtract).then_inc(pl_done, 1)

            for j in range(1, EARLY):
                split_early(j)

            for i in range(STEPS):
                if 0 <= i - HI_LAG < NH:
                    prob_lo(i - HI_LAG, 0)
                    if lo_tiles(i - HI_LAG) > 0:
                        prob_lo(i - HI_LAG, 1)
                for b, s in tail_of(i - 1):
                    if s == TAIL_WO:
                        t = NT + QT * b
                        pool.wait_ge(var_ready, 2 + b)
                        nc.gpsimd.tensor_tensor(rstd[:, t:t + QT], vare[:, t:t + QT], c_mhalf[:, t:t + QT],
                                                ALU.pow).then_inc(rstd_ready, 1)
                    if s == TAIL_GATE:
                        pool.wait_ge(gexp_go, b + 1)
                        nc.gpsimd.tensor_tensor(gexp[:, QT * b:QT * b + QT], c_e[:, :],
                                                gdiff[:, QT * b:QT * b + QT], ALU.pow).then_inc(gexp_done, 1)
                k = i - FFN0 - 1
                if 0 <= k < NF:
                    pool.wait_ge(hh_done, k + 1)
                    nc.gpsimd.tensor_tensor(hid_lo[:, k % 2, :], hid[:, k % 2, :], hid_hi[:, k % 2, :],
                                            ALU.subtract).then_inc(hl_done, 1)

        @block.scalar
        def _(act):
            def split_a(w):
                act.wait_ge(ld_w[w], 16)
                nc.scalar.activation(wa[:, 0, w, :], ring_a(w), ACT.Copy, scale=S_W).then_inc(w_hi, 1)

            def tanh_gates():
                act.wait_ge(ld_small, 48)
                nc.scalar.activation(gates[:, 2:4], gates[:, 0:2], ACT.Tanh).then_inc(tanh_done, 1)

            def item_of(n):
                item = ITEMS[n]
                for w in SPLIT_BEFORE.get(n, []):
                    split_a(w)
                if n == 8:
                    tanh_gates()
                act.wait_ge(item_ps, n + 1)
                src = item_out(n)
                kind = item[0]
                if kind == "tx":
                    dst, s = xT[:, 0, :], S_ACTV
                elif kind == "tc":
                    dst, s = cT[:, 0, item[1] * T2:(item[1] + 1) * T2], S_ACTV
                elif kind == "k":
                    _, b, p = item
                    if b > 0:
                        act.wait_ge(k_st[group_of(0, p)], 64)
                    dst, s = k_nat[:, 0, p, :], 1.0 / S_W
                elif kind == "q":
                    dst, s = q_nat[:, 0, item[1], :], 1.0 / S_W
                else:
                    _, b, t = item
                    dst, s = v_hi[:, b * KT + t, :, 0:DH], 1.0 / S_W
                    src = src.rearrange("p (h d) -> p h d", d=DH)
                nc.scalar.activation(dst, src, ACT.Copy, scale=s).then_inc(item_hi, 1)

            for n in range(NI - LATE):
                item_of(n)

            def exp_half(j, g):
                act.wait_ge(score_ps, 2 * j + g + 1)
                if j >= 2:
                    act.wait_ge(pl_done, pool_lo(j - 2, g))
                    if g == 1:
                        act.wait_ge(pd_done, j - 1)
                nc.scalar.activation(prob[:, j % 2, g, :], span(2 + 2 * g, 3 * T1), ACT.Exp,
                                     scale=DH ** -0.5 / S_SCORE).then_inc(exp_done, 1)

            for i in range(STEPS):
                for q in range(QT):
                    for n in late_items(i, q):
                        item_of(n)
                for b, s in tail_of(i - 1):
                    if s in (TAIL_O0, TAIL_O1):
                        act.wait_ge(misc_ps, MISC[(s, b)] + 1)
                        t = QT * b + s
                        nc.scalar.activation(oT[:, 0, t, :], misc, ACT.Copy, scale=S_ACTV).then_inc(misc_hi, 1)
                    if s == TAIL_X:
                        act.wait_ge(misc_ps, MISC[(s, b)] + 1)
                        nc.scalar.activation(x2h[:, 0, b * T1:(b + 1) * T1], misc[:, 0:T1], ACT.Copy,
                                             scale=S_ACTV).then_inc(misc_hi, 1)
                j = i - ST_LAG
                if 0 <= j < NH:
                    exp_half(j, 0)
                if 0 <= j < NH:
                    act.wait_ge(exp_done, 2 * j + 1)
                    if j >= 3:
                        act.wait_ge(pv_ps, QT * (j - 2))
                    nc.scalar.activation(p_hi[:, j % 3, 0:3, :].rearrange("p t n -> p (t n)"), prob[:, j % 2, 0, :],
                                         ACT.Copy).then_inc(ph_act, 1)
                if 1 <= i <= NH:
                    act.wait_ge(misc_ps, MISC[("shift", i - 1)] + 1)
                    b, h = divmod(i - 1, HEADS)
                    nc.scalar.activation(q_b[DH:DH + 1, place(h), b * T1:(b + 1) * T1], misc[DH:DH + 1, 0:T1],
                                         ACT.Copy).then_inc(shift_done, 1)
                if 0 <= j < NH:
                    exp_half(j, 1)
                k = i - FFN0
                if 0 <= k < NF:
                    e = EORDER[k % NE]
                    if k >= 2:
                        act.wait_ge(hl_done, k - 1)
                    for c in range(HC):
                        act.wait_ge(h_ps, HC // 2 * k + c // 2 + 1)
                        nc.scalar.activation(hid[:, k % 2, c * T1:(c + 1) * T1],
                                             span(2 * (k % 2), HC * T1)[:, c * T1:(c + 1) * T1], ACT.Gelu,
                                             bias=b1T[:, e * HC + c:e * HC + c + 1],
                                             scale=1.0 / (S_ACTV * S_W)).then_inc(gelu_done, 1)
                j = i - FSPLIT0
                if EARLY <= j < NE:
                    act.wait_ge(ld_f[j], 32)
                    nc.scalar.activation(wf[:, 0, EORDER[j], :, :], ring_f(j), ACT.Copy, scale=S_W).then_inc(f_hi, 1)

        @block.vector
        def _(dve):
            n_chain = 0
            n_mhi = 0

            def mark(ins):
                nonlocal n_chain
                n_chain += 1
                ins.then_inc(dve_chain, 1)

            def settle():
                dve.wait_ge(dve_chain, n_chain)

            def link(ins):
                mark(ins)
                settle()

            def row_statistics(src, first, tiles):
                for t in range(tiles):
                    mark(nc.vector.bn_stats(stats[:, first + t, :], src[:, t, :]))
                settle()
                for t in range(tiles):
                    mark(nc.vector.bn_aggr(mv[:, first + t, :], stats[:, first + t, :]))
                settle()
                nc.vector.tensor_scalar(vare[:, first:first + tiles], mv[:, first:first + tiles, 1], EPS, None,
                                        ALU.add).then_inc(var_ready, 1)

            def normalise_rows(src, first, tiles, phase):
                dve.wait_ge(rstd_ready, phase)
                for t in range(tiles):
                    nc.vector.tensor_scalar(xn[:, (first + t) % NT, :], src[:, t, :], mv[:, first + t, 0:1],
                                            rstd[:, first + t:first + t + 1], ALU.subtract,
                                            ALU.mult).then_inc(xn_ready, 1)

            def split_a(w):
                dve.wait_ge(w_hi, SPLIT_AT[w])
                nc.vector.scalar_tensor_tensor(out=wa[:, 1, w, :], in0=ring_a(w), scalar=S_W, in1=wa[:, 0, w, :],
                                               op0=ALU.mult, op1=ALU.subtract).then_inc(w_lo, 1)

            def item_of(n):
                item = ITEMS[n]
                if item[0] == "tx":
                    normalise_rows(x_sb, 0, NT, 1)
                for w in SPLIT_BEFORE.get(n, []):
                    split_a(w)
                dve.wait_ge(item_hi, n + 1)
                src = item_out(n)
                kind = item[0]
                if kind == "tx":
                    dst, hi, s = xT[:, 1, :], xT[:, 0, :], S_ACTV
                elif kind == "tc":
                    cols = slice(item[1] * T2, (item[1] + 1) * T2)
                    dst, hi, s = cT[:, 1, cols], cT[:, 0, cols], S_ACTV
                elif kind == "k":
                    p = item[2]
                    dst, hi, s = k_nat[:, 1, p, :], k_nat[:, 0, p, :], 1.0 / S_W
                elif kind == "q":
                    p = item[1]
                    dst, hi, s = q_nat[:, 1, p, :], q_nat[:, 0, p, :], 1.0 / S_W
                else:
                    t = item[1] * KT + item[2]
                    dst, hi, s = v_lo[:, t, :, :], v_hi[:, t, :, 0:DH], 1.0 / S_W
                    src = src.rearrange("p (h d) -> p h d", d=DH)
                nc.vector.scalar_tensor_tensor(out=dst, in0=src, scalar=s, in1=hi, op0=ALU.mult,
                                               op1=ALU.subtract).then_inc(item_lo, 1)

            dve.wait_ge(ld_x, 16)
            row_statistics(x_sb, 0, NT)
            for n in range(NI - LATE):
                item_of(n)

            dve.wait_ge(tanh_done, 1)
            mark(nc.vector.tensor_scalar(scales[:, 0:1], gates[:, 2:3], 1.0 / (S_ACTV * S_W), None, ALU.mult))
            mark(nc.vector.tensor_scalar(scales[:, 1:2], gates[:, 3:4], 1.0 / S_W, None, ALU.mult))

            def take_max(i, q):
                dve.wait_ge(max_ps, QT * i + q + 1)
                nc.vector.tensor_reduce(nmax[:, i, q:q + 1], span(0, KEYS), AX_X, ALU.max,
                                        negate=True).then_inc(max_done, 1)

            def normalise(j):
                dve.wait_ge(pv_ps, QT * (j + 1))
                b, h = divmod(j, HEADS)
                link(nc.vector.reciprocal(rsum[:, j, :], o_ps[:, :, DH]))
                nc.vector.tensor_tensor(o_sb[:, QT * b:QT * b + QT, h * DH:(h + 1) * DH], o_ps[:, :, 0:DH],
                                        rsum[:, j, :].unsqueeze(2).broadcast_to([P, QT, DH]),
                                        ALU.mult).then_inc(o_done, 1)

            def lo_of_misc(dst, hi, n):
                nc.vector.scalar_tensor_tensor(out=dst, in0=misc[:, 0:n], scalar=S_ACTV, in1=hi, op0=ALU.mult,
                                               op1=ALU.subtract).then_inc(misc_done, 1)

            def tail_first(b, s):
                tiles = slice(QT * b, QT * b + QT)
                if s == TAIL_X:
                    normalise_rows(acc[:, tiles, :], NT + QT * b, QT, 2 + b)
                if s == TAIL_COMB:
                    dve.wait_ge(gexp_done, b + 1)
                    link(nc.vector.tensor_scalar(gsum[:, tiles], gexp[:, tiles], 1.0, None, ALU.add))
                    link(nc.vector.reciprocal(gtop[:, tiles, 0], gsum[:, tiles]))
                    mark(nc.vector.tensor_tensor(gtop[:, tiles, 1], gtop[:, tiles, 0], gexp[:, tiles], ALU.mult))
                    link(nc.vector.tensor_tensor(first[:, tiles, :], first[:, tiles, :],
                                                 gtop[:, tiles, 0:1].broadcast_to([P, QT, E]), ALU.mult))
                    link(nc.vector.tensor_tensor(first[:, tiles, :], first[:, tiles, :],
                                                 gtop[:, tiles, 1:2].broadcast_to([P, QT, E]), ALU.max))
                    link(nc.vector.tensor_tensor(comb[:, tiles, 0:E], first[:, tiles, :], mask[:, tiles, :],
                                                 ALU.mult))
                    nc.vector.tensor_scalar(comb_s[:, tiles, :], comb[:, tiles, :], scales[:, 1:2], None,
                                            ALU.mult).then_inc(comb_ready, 1)
                    dve.wait_ge(comb_ready, b + 1)

            def tail(b, s):
                nonlocal n_mhi
                tiles = slice(QT * b, QT * b + QT)
                cols = slice(b * T1, (b + 1) * T1)
                dve.wait_ge(misc_ps, MISC[(s, b)] + 1)
                if s in (TAIL_O0, TAIL_O1, TAIL_X):
                    n_mhi += 1
                    dve.wait_ge(misc_hi, n_mhi)
                if s in (TAIL_O0, TAIL_O1):
                    t = QT * b + s
                    lo_of_misc(oT[:, 1, t, :], oT[:, 0, t, :], INNER)
                elif s == TAIL_WO:
                    dve.wait_ge(xb_done, NT)
                    nc.vector.scalar_tensor_tensor(
                        out=acc[:, tiles, :].rearrange("p t d -> p (t d)"), in0=misc[:, 0:QT * D],
                        scalar=scales[:, 0:1], in1=x_sb[:, tiles, :].rearrange("p t d -> p (t d)"),
                        op0=ALU.mult, op1=ALU.add).then_inc(misc_done, 1)
                    dve.wait_ge(misc_done, MISC[(s, b)] + 1 - shifts_before(MISC[(s, b)]))
                    row_statistics(acc[:, tiles, :], NT + QT * b, QT)
                elif s == TAIL_X:
                    link(nc.vector.tensor_copy(x2T[:, cols], misc[:, 0:T1]))
                    lo_of_misc(x2h[:, 1, cols], x2h[:, 0, cols], T1)
                elif s == TAIL_GATE:
                    nc.vector.tensor_tensor(logit[:, tiles, 0:E], misc[:, 0:QT * E].rearrange("p (t e) -> p t e", e=E),
                                            gb[:, :].unsqueeze(1).broadcast_to([P, QT, E]),
                                            ALU.add).then_inc(misc_done, 1)
                    dve.wait_ge(misc_done, MISC[(s, b)] + 1 - shifts_before(MISC[(s, b)]))
                    for t in range(QT * b, QT * b + QT):
                        mark(nc.vector.max(top8[:, t, :], logit[:, t, 0:E]))
                    settle()
                    mark(nc.vector.tensor_copy(pick8[:, tiles, 0:2], top8[:, tiles, 0:2]))
                    nc.vector.tensor_tensor(gdiff[:, tiles], top8[:, tiles, 1], top8[:, tiles, 0],
                                            ALU.subtract).then_inc(gexp_go, 1)
                    mark(nc.vector.tensor_tensor(first[:, tiles, :], logit[:, tiles, 0:E],
                                                 top8[:, tiles, 0:1].broadcast_to([P, QT, E]), ALU.is_equal))
                    settle()
                    for t in range(QT * b, QT * b + QT):
                        mark(nc.vector.match_replace(marked[:, t, :], pick8[:, t, :], logit[:, t, :], PICKED))
                    settle()
                    mark(nc.vector.tensor_scalar(mask[:, tiles, :], marked[:, tiles, 0:E], PICKED, None,
                                                 ALU.is_equal))
                elif s == TAIL_COMB:
                    nc.vector.tensor_copy(combT[:, cols], misc[0:NE, 0:T1]).then_inc(misc_done, 1)
                elif s == TAIL_B2:
                    nc.vector.scalar_tensor_tensor(
                        out=acc[:, tiles, :].rearrange("p t d -> p (t d)"), in0=misc[:, 0:QT * D],
                        scalar=gates[:, 3:4], in1=acc[:, tiles, :].rearrange("p t d -> p (t d)"),
                        op0=ALU.mult, op1=ALU.add).then_inc(misc_done, 1)
                    dve.wait_ge(misc_done, MISC[(s, b)] + 1 - shifts_before(MISC[(s, b)]))

            def second_half(j):
                dve.wait_ge(exp_done, 2 * j + 2)
                if j >= 3:
                    dve.wait_ge(pv_ps, QT * (j - 2))
                nc.vector.tensor_copy(p_hi[:, j % 3, 3:6, :].rearrange("p t n -> p (t n)"),
                                      prob[:, j % 2, 1, :]).then_inc(ph_dve, 1)
                dve.wait_ge(ph_dve, j + 1)
                n = lo_tiles(j)
                nc.vector.tensor_tensor(p_lo[:, j % 3, 3 + n:6, :].rearrange("p t n -> p (t n)"),
                                        prob[:, j % 2, 1, n * T1:],
                                        p_hi[:, j % 3, 3 + n:6, :].rearrange("p t n -> p (t n)"),
                                        ALU.subtract).then_inc(pd_done, 1)

            for i in range(STEPS):
                if 0 <= i - NORM_LAG < NH:
                    normalise(i - NORM_LAG)
                k = i - FFN0 - 1
                if 0 <= k < NF:
                    dve.wait_ge(gelu_done, HC * (k + 1))
                    if k >= 2:
                        dve.wait_ge(y_ps, k - 1)
                    nc.vector.tensor_copy(hid_hi[:, k % 2, :], hid[:, k % 2, :]).then_inc(hh_done, 1)
                if i < NH:
                    take_max(i, 0)
                for n in late_items(i, 0):
                    item_of(n)
                for b, s in tail_of(i - 1):
                    tail(b, s)
                for b, s in tail_of(i):
                    tail_first(b, s)
                if 0 <= i - HI_LAG < NH:
                    second_half(i - HI_LAG)
                if i < NH:
                    take_max(i, 1)
                    dve.wait_ge(max_done, QT * (i + 1))
                    nc.vector.tensor_scalar(shift16[:, i, :], nmax[:, i, :], 1.0 / SHIFT_ROW, SHIFT_P, ALU.mult,
                                            ALU.add).then_inc(shift_ready, 1)
                for n in late_items(i, 1):
                    item_of(n)
                k = i - FFN0 - 3
                if 0 <= k < NF:
                    b, e = k // NE, EORDER[k % NE]
                    dve.wait_ge(y_ps, k + 1)
                    for t in range(QT):
                        ins = nc.vector.scalar_tensor_tensor(
                            out=acc[:, QT * b + t, :], in0=banks[:, 4 + k % 2, t * D:(t + 1) * D],
                            scalar=comb_s[:, QT * b + t, e:e + 1], in1=acc[:, QT * b + t, :],
                            op0=ALU.mult, op1=ALU.add)
                        if t < QT - 1:
                            link(ins)
                    ins.then_inc(y_done, 1)
                    dve.wait_ge(y_done, k + 1)
                j = i - FSPLIT0 - 1
                if EARLY <= j < NE:
                    dve.wait_ge(f_hi, j - EARLY + 1)
                    e = EORDER[j]
                    nc.vector.scalar_tensor_tensor(
                        out=wf[:, 1, e, :, :].rearrange("p a n -> p (a n)"),
                        in0=ring_f(j).rearrange("p a n -> p (a n)"), scalar=S_W,
                        in1=wf[:, 0, e, :, :].rearrange("p a n -> p (a n)"),
                        op0=ALU.mult, op1=ALU.subtract).then_inc(f_lo, 1)
                if i == BIAS_STEP:
                    dve.wait_ge(misc_ps, MISC[("b1", 0)] + 1)
                    nc.vector.tensor_copy(b1T[:, :], misc[:, 0:NE * HC]).then_inc(misc_done, 1)

        @block.tensor
        def _(pe):
            def three(dst, w, a, start=True, stop=True):
                nc.tensor.matmul(dst, w[0], a[0], start=start, stop=False)
                nc.tensor.matmul(dst, w[0], a[1], start=False, stop=False)
                return nc.tensor.matmul(dst, w[1], a[0], start=False, stop=stop)

            def w_pair(w, cols):
                return wa[:, 0, w, cols], wa[:, 1, w, cols]

            def x_pair(cols):
                return xT[:, 0, cols], xT[:, 1, cols]

            def c_pair(cols):
                return cT[:, 0, cols], cT[:, 1, cols]

            pe.wait_ge(consts, 3)
            def item_of(n):
                item = ITEMS[n]
                kind = item[0]
                dst = item_out(n)
                if before(n, SLOT[n]) > 0:
                    pe.wait_ge(item_lo, before(n, SLOT[n]))
                if kind == "tx":
                    for t in range(NT):
                        pe.wait_ge(xn_ready, t + 1)
                        last = nc.tensor.transpose(dst[:, t * P:(t + 1) * P], xn[:, t, :], ident[:, :])
                elif kind == "tc":
                    b = item[1]
                    pe.wait_ge(ld_ctx[b], 16)
                    for t in range(T2 // P):
                        last = nc.tensor.transpose(dst[:, t * P:(t + 1) * P], ctx_sb[:, b * (T2 // P) + t, :],
                                                   ident[:, :])
                elif kind == "k":
                    _, b, p = item
                    pair = slice(p * P, (p + 1) * P)
                    pe.wait_ge(w_lo, SPLIT_AT[WK1])
                    pe.wait_ge(item_lo, ITEMS.index(("tc", b)) + 1)
                    pe.wait_ge(item_lo, ITEMS.index(("tx", 0)) + 1)
                    three(dst[:, 0:T2], w_pair(WK2, pair), c_pair(slice(b * T2, (b + 1) * T2)))
                    last = three(dst[:, T2:KEYS], w_pair(WK1, pair), x_pair(slice(b * T1, (b + 1) * T1)))
                elif kind == "q":
                    p = item[1]
                    pe.wait_ge(w_lo, SPLIT_AT[WQ])
                    last = three(dst, w_pair(WQ, slice(p * P, (p + 1) * P)), x_pair(slice(0, B * T1)))
                else:
                    _, b, t = item
                    if t < T2 // P:
                        pe.wait_ge(w_lo, SPLIT_AT[WV2])
                        pe.wait_ge(item_lo, ITEMS.index(("tc", b)) + 1)
                        last = three(dst, c_pair(ctx_cols(b, t)), w_pair(WV2, slice(0, INNER)))
                    else:
                        pe.wait_ge(w_lo, SPLIT_AT[WV1])
                        at = b * T1 + (t - T2 // P) * P
                        last = three(dst, x_pair(slice(at, at + P)), w_pair(WV1, slice(0, INNER)))
                last.then_inc(item_ps, 1)

            for n in range(NI - LATE):
                item_of(n)

            def max_scores(i, q):
                b, h = divmod(i, HEADS)
                if q == 0:
                    pe.wait_ge(k_st[b * PAIRS + group_of(b, h // 2)], 64)
                    pe.wait_ge(q_st[group_of(0, h // 2)], 64)
                if i + q > 0:
                    pe.wait_ge(max_done, QT * i + q)
                h = place(h)
                queries = q_a[0:DH, h, b * T1 + q * P:b * T1 + (q + 1) * P]
                nc.tensor.matmul(span(0, KEYS)[:, 0:T2], queries, k_a[0:DH, h, 0:T2], start=True, stop=True)
                nc.tensor.matmul(span(0, KEYS)[:, T2:KEYS], queries, k_a[0:DH, h, T2:KEYS], start=True,
                                 stop=True).then_inc(max_ps, 1)

            def scores(j, g):
                b, h = divmod(j, HEADS)
                if g == 0:
                    pe.wait_ge(shift_done, j + 1)
                if j >= 1:
                    pe.wait_ge(exp_done, 2 * (j - 1) + g + 1)
                h = place(h)
                dst = span(2 + 2 * g, 3 * T1)
                queries = slice(b * T1, (b + 1) * T1)
                for n in range(3):
                    t = 3 * g + n
                    keys = slice(t * P, (t + 1) * P)
                    cols = slice(n * T1, (n + 1) * T1)
                    nc.tensor.matmul(dst[:, cols], k_a[:, h, keys], q_a[:, h, queries], start=True, stop=False)
                    last = nc.tensor.matmul(dst[:, cols], k_b[0:DH + 1, h, keys], q_b[0:DH + 1, h, queries],
                                            start=False, stop=True)
                last.then_inc(score_ps, 1)

            def bank7_free(use):
                n = MISC[use]
                shifts = shifts_before(n)
                if shifts > 0:
                    pe.wait_ge(shift_done, shifts)
                if n - shifts > 0:
                    pe.wait_ge(misc_done, n - shifts)

            def shift_row(i):
                pe.wait_ge(shift_ready, i + 1)
                bank7_free(("shift", i))
                for q in range(QT):
                    last = nc.tensor.matmul(misc[DH:DH + 1, q * P:(q + 1) * P], shift16[:, i, q:q + 1],
                                            ident16[:, :], start=True, stop=True)
                last.then_inc(misc_ps, 1)

            def values(j, q):
                b, h = divmod(j, HEADS)
                if q == 0:
                    pe.wait_ge(pl_done, pool_lo(j, 0))
                    if j >= 1:
                        pe.wait_ge(o_done, j)
                cols = slice(q * P, (q + 1) * P)
                for t in range(KT):
                    if q == 0 and t == KT // 2:
                        pe.wait_ge(pl_done, pool_lo(j, 1))
                        pe.wait_ge(pd_done, j + 1)
                    vh, vl = v_hi[:, b * KT + t, h, :], v_lo[:, b * KT + t, h, :]
                    ph, pl = p_hi[:, j % 3, t, cols], p_lo[:, j % 3, t, cols]
                    nc.tensor.matmul(o_ps[:, q, :], ph, vh, start=(t == 0), stop=False, skip_group_check=True)
                    nc.tensor.matmul(o_ps[:, q, 0:DH], ph, vl, start=False, stop=False, skip_group_check=True)
                    last = nc.tensor.matmul(o_ps[:, q, :], pl, vh, start=False, stop=(t == KT - 1),
                                            skip_group_check=True)
                last.then_inc(pv_ps, 1)

            def tail(b, s):
                bank7_free((s, b))
                if s in (TAIL_O0, TAIL_O1):
                    pe.wait_ge(o_done, HEADS * (b + 1))
                    for c in range(INNER // P):
                        last = nc.tensor.transpose(misc[:, c * P:(c + 1) * P],
                                                   o_sb[:, QT * b + s, c * P:(c + 1) * P], ident[:, :])
                elif s == TAIL_WO:
                    for q in range(QT):
                        t = QT * b + q
                        for c in range(INNER // P):
                            cols = slice(c * P, (c + 1) * P)
                            last = three(misc[:, q * D:(q + 1) * D], (oT[:, 0, t, cols], oT[:, 1, t, cols]),
                                         w_pair(WO, cols), start=(c == 0), stop=(c == INNER // P - 1))
                elif s == TAIL_X:
                    pe.wait_ge(xn_ready, NT + QT * (b + 1))
                    for q in range(QT):
                        last = nc.tensor.transpose(misc[:, q * P:(q + 1) * P], xn[:, QT * b + q, :], ident[:, :])
                elif s == TAIL_GATE:
                    pe.wait_ge(ld_rows, 96)
                    for q in range(QT):
                        at = b * T1 + q * P
                        last = nc.tensor.matmul(misc[:, q * E:(q + 1) * E], x2T[:, at:at + P], gw[:, :],
                                                start=True, stop=True)
                elif s == TAIL_COMB:
                    pe.wait_ge(comb_ready, b + 1)
                    for q in range(QT):
                        last = nc.tensor.transpose(misc[0:NE, q * P:(q + 1) * P], comb[:, QT * b + q, :],
                                                   ident[:, :])
                else:
                    for q in range(QT):
                        at = b * T1 + q * P
                        last = nc.tensor.matmul(misc[:, q * D:(q + 1) * D], combT[:, at:at + P], b2_rows[:, :],
                                                start=True, stop=True)
                last.then_inc(misc_ps, 1)

            for i in range(STEPS):
                k = i - FFN0
                if 0 <= k < NF:
                    b, e = k // NE, EORDER[k % NE]
                    if k == 0:
                        pe.wait_ge(max_done, QT * NH)
                    if k == 1:
                        pe.wait_ge(exp_done, 2 * NH)
                    if k >= 2:
                        pe.wait_ge(gelu_done, HC * (k - 1))
                    if k < EARLY:
                        pe.wait_ge(e_lo, k + 1)
                    elif k < NE:
                        pe.wait_ge(f_lo, k - EARLY + 1)
                    if k % NE == 0:
                        n = MISC[(TAIL_X, b)] + 1
                        pe.wait_ge(misc_done, n - shifts_before(n))
                    tok = slice(b * T1, (b + 1) * T1)
                    for c in range(HC):
                        cols = slice(c * P, (c + 1) * P)
                        last = three(span(2 * (k % 2), HC * T1)[:, c * T1:(c + 1) * T1],
                                     (wf[:, 0, e, 0, cols], wf[:, 1, e, 0, cols]),
                                     (x2h[:, 0, tok], x2h[:, 1, tok]))
                        if c % 2 == 1:
                            last.then_inc(h_ps, 1)
                if i < NH:
                    if i == 0:
                        pe.wait_ge(item_lo, before(NI, 0))
                        pe.wait_ge(consts, 8)
                    max_scores(i, 0)
                if 0 <= i - ST_LAG < NH:
                    if i == ST_LAG:
                        pe.wait_ge(item_lo, NI)
                    scores(i - ST_LAG, 0)
                if 0 <= i - PV_LAG < NH:
                    values(i - PV_LAG, 0)
                for n in late_items(i, 0):
                    item_of(n)
                if i < NH:
                    max_scores(i, 1)
                if 1 <= i <= NH:
                    if i == 1:
                        pe.wait_ge(item_lo, before(NI, 3))
                    shift_row(i - 1)
                for n in late_items(i, 1):
                    item_of(n)
                if 0 <= i - ST_LAG < NH:
                    scores(i - ST_LAG, 1)
                if 0 <= i - PV_LAG < NH:
                    values(i - PV_LAG, 1)
                k = i - FFN0 - 2
                if 0 <= k < NF:
                    e = EORDER[k % NE]
                    pe.wait_ge(hl_done, k + 1)
                    if k >= 2:
                        pe.wait_ge(y_done, k - 1)
                    for q in range(QT):
                        for c in range(HC):
                            at = c * T1 + q * P
                            cols = slice(c * P, (c + 1) * P)
                            last = three(banks[:, 4 + k % 2, q * D:(q + 1) * D],
                                         (hid_hi[:, k % 2, at:at + P], hid_lo[:, k % 2, at:at + P]),
                                         (wf[:, 0, e, 1, cols], wf[:, 1, e, 1, cols]),
                                         start=(c == 0), stop=(c == HC - 1))
                    last.then_inc(y_ps, 1)
                if i == BIAS_STEP:
                    pe.wait_ge(ld_rows, 96)
                    bank7_free(("b1", 0))
                    nc.tensor.transpose(misc[:, 0:NE * HC], b1_rows[:, :],
                                        ident[0:NE * HC, 0:NE * HC]).then_inc(misc_ps, 1)
                for b, s in tail_of(i):
                    tail(b, s)


_INS = ['x', 'ctx_1024', 'g_xattn', 'g_ffn', 'L0_xattn_Wq1', 'L0_xattn_Wk1', 'L0_xattn_Wv1', 'L0_xattn_Wk2',
        'L0_xattn_Wv2', 'L0_xattn_Wo', 'L0_xattn_bo', 'L0_ffn_gate_w', 'L0_ffn_gate_b', 'L0_ffn_w1', 'L0_ffn_b1',
        'L0_ffn_w2', 'L0_ffn_b2', 'L0_ffn_ws1', 'L0_ffn_bs1', 'L0_ffn_ws2', 'L0_ffn_bs2']
_OUTS = [((B, T1, D), 'float32')]


def kernel(**inputs):
    import numpy as _np
    import concourse.bacc as _bacc
    from concourse import mybir as _mybir
    from concourse.bass_utils import run_bass_kernel_spmd as _run

    nc = _bacc.Bacc("TRN2", target_bir_lowering=False, num_devices=1)
    arrays, args = {}, []
    for name in _INS:
        a = _np.ascontiguousarray(inputs[name])
        arrays[f"in_{name}_dram"] = a
        args.append(nc.dram_tensor(f"in_{name}_dram", a.shape, _mybir.dt.from_np(a.dtype), kind="ExternalInput").ap())
    for i, (shape, dtype) in enumerate(_OUTS):
        dt = _mybir.dt.from_np(_np.dtype(dtype))
        args.append(nc.dram_tensor(f"out_{i}_dram", shape, dt, kind="ExternalOutput").ap())
    block_kernel(nc, *args)
    r = _run(nc, [arrays], core_ids=[0])
    got = tuple(r.results[0][f"out_{i}_dram"] for i in range(len(_OUTS)))
    return got[0]
```

```python
from contextlib import ExitStack
from math import log
from struct import pack, unpack

import concourse.bass as bass
from concourse import mybir

F32 = mybir.dt.float32
F16 = mybir.dt.float16
ALU = mybir.AluOpType
ACT = mybir.ActivationFunctionType
AX_X = mybir.AxisListType.X

P = 128
B = 2
T1 = 256
T2 = 512
D = 128
HEADS = 8
DH = 64
INNER = HEADS * DH
PAIRS = HEADS // 2
KEYS = T1 + T2
KT = KEYS // P
QT = T1 // P
NT = B * QT
NH = B * HEADS
E = 8
NE = E + 1
HID = 512
HC = HID // P
NW = 6
WK2, WK1, WQ, WV2, WV1, WO = range(NW)
RING = 4
EORDER = [E] + list(range(E))
EPS = 1e-5

S_ACTV = 64.0
S_W = 1024.0
S_SCORE = S_ACTV * S_ACTV
SHIFT_ROW = S_SCORE
SHIFT_PAIR, = unpack("<f", pack("<ee", SHIFT_ROW, SHIFT_ROW))
P_SCALE = S_ACTV
SHIFT_P = log(P_SCALE) * DH ** 0.5
NONE = -3.0e38
PICKED = 3.0e38

ST_LAG = 2
HI_LAG = 3
PV_LAG = 4
FFN0 = NH + ST_LAG
NF = B * NE
STEPS = FFN0 + NF + 4
TAIL0 = [HEADS + PV_LAG, NH + PV_LAG + 1]
BIAS_STEP = 10
EARLY = 3
FSPLIT0 = 15
TAIL_O0, TAIL_O1, TAIL_WO, TAIL_X, TAIL_GATE, TAIL_COMB, TAIL_B2 = TAIL_STAGES = (0, 1, 2, 4, 5, 7, 8)


def late_items(i, q):
    if i >= len(LATE_PLAN):
        return range(0)
    counts = [c for step in LATE_PLAN for c in step]
    n = NI - LATE + sum(counts[:2 * i + q])
    return range(n, n + counts[2 * i + q])


def place(h):
    return h % 2 * PAIRS + h // 2


def tail_of(i):
    return [(b, i - TAIL0[b]) for b in range(B) if i - TAIL0[b] in TAIL_STAGES]


def plan_items():
    items = [("tc", 0), ("tx", 0)]
    for p in range(PAIRS):
        items += [("k", 0, p), ("q", p)]
    items += [("v", 0, 0), ("tc", 1)]
    items += [("v", 0, t) for t in range(1, KT)]
    items += [("v", 1, t) for t in range(KT - LAST_V)]
    items += [("k", 1, p) for p in range(PAIRS)]
    items += [("v", 1, t) for t in range(KT - LAST_V, KT)]
    return items


LAST_V = 2
ITEMS = plan_items()
NI = len(ITEMS)
WARM_START, WARM_LAYERNORM, WARM_STEP = 14, 9, 8
LATE_PLAN = [(2, 2), (2, 1), (0, 1), (0, 1)]
LATE_SLOT = [1, 2, 3, 1, 2, 1, 2, 3, 3]
LATE = len(LATE_SLOT)
SLOT = [(n - (NI - LATE)) % 4 for n in range(NI - LATE)] + LATE_SLOT


def before(n, slot):
    return max([m + 1 for m in range(n) if SLOT[m] == slot], default=0)


SPLIT_BEFORE = {1: [WK2, WK1], 2: [WQ], 5: [WV2], 8: [WV1], 10: [WO]}
SPLIT_ORDER = [w for n in sorted(SPLIT_BEFORE) for w in SPLIT_BEFORE[n]]
BY_POOL = [WV2, WO]
SPLIT_AT = {w: sum(1 for v in SPLIT_ORDER[:SPLIT_ORDER.index(w) + 1] if v not in BY_POOL) for w in SPLIT_ORDER}


GROUPS = [[(0, 1), (1, PAIRS)], [(0, 2), (2, PAIRS)]]


def group_of(b, p):
    return max(p0 for p0, _ in GROUPS[b] if p0 <= p)


LO_LAST = NH - 1


def lo_tiles(j):
    return 2 if j < LO_LAST else 0


def pool_lo(j, g):
    return 2 * j + g + 1 - max(0, j - LO_LAST + (g == 1)) if j >= 0 else 0


HB = 3
SHARED_LO = range(NF - 1, NF)


def shared(k):
    return sum(1 for m in SHARED_LO if m < k)


def hi_count(k):
    return k + shared(k)


def hid_parts(k):
    return [(0, HC // 2), (HC // 2, HC)] if k in SHARED_LO else [(0, HC)]


def shifts_before(n):
    return sum(1 for u, m in MISC.items() if m < n and u[0] == "shift")


def plan_misc():
    uses = []
    for i in range(STEPS):
        if 1 <= i <= NH:
            uses.append(("shift", i - 1))
        if i == BIAS_STEP:
            uses.append(("b1", 0))
        for b, s in tail_of(i):
            uses.append((s, b))
    return {u: n for n, u in enumerate(uses)}


MISC = plan_misc()


def block_kernel(nc, x, ctx_in, g_xattn, g_ffn, Wq1, Wk1, Wv1, Wk2, Wv2, Wo, bo,
                 gate_w, gate_b, w1, b1, w2, b2, ws1, bs1, ws2, bs2, out):
    stack = ExitStack()
    with stack:
        def sb(name, shape, dt):
            return stack.enter_context(nc.sbuf_tensor(name, shape, dt))

        def sem(name):
            return stack.enter_context(nc.semaphore(name))

        x_sb = sb("x_sb", [P, NT, D], F32)
        prob_all = sb("prob", [P, 4 * (KEYS // 2) * QT], F32)
        ctx_sb = prob_all[:, 0:B * T2 // P * D].rearrange("p (t d) -> p t d", d=D)
        prob = prob_all[:, :].rearrange("p (a g n) -> p a g n", a=2, g=2)
        xT = sb("xT", [P, 2, B * T1], F16)
        cT = sb("cT", [P, 2, B * T2], F16)
        ring = sb("ring", [P, RING, 2, 512], F32)
        wa = sb("wa", [P, 2, NW, 512], F16)
        wf = sb("wf", [P, 2, NE, 2, 512], F16)
        kab = sb("kab", [P, 2, HEADS, KEYS], F16)
        k_a = kab[:, 0]
        k_b = kab[:, 1]
        kflat = kab[:, :, :, :].rearrange("p a h n -> p (a h n)")
        hid = kflat[:, 0:4096].bitcast(F32).rearrange("p (u n) -> p u n", u=2)
        hid_hi = kflat[:, 4096:7168].rearrange("p (u n) -> p u n", u=HB)
        hid_lo = kflat[:, 7168:10240].rearrange("p (u n) -> p u n", u=HB)
        k_nat = sb("k_nat", [P, 2, PAIRS, KEYS], F16)
        qab = sb("qab", [P, 2, HEADS, B * T1], F16)
        q_a = qab[:, 0]
        q_b = qab[:, 1]
        qo = sb("qo", [P, 2, 4, 512], F16)
        q_nat = qo
        oT = qo
        v_hi = sb("v_hi", [P, B * KT, HEADS, DH + 1], F16)
        v_lo = sb("v_lo", [P, B * KT, HEADS, DH], F16)
        p_hi = sb("p_hi", [P, 3, KT, T1], F16)
        p_lo = sb("p_lo", [P, 3, KT, T1], F16)
        o_sb = sb("o_sb", [P, NT, INNER], F32)
        xn = sb("xn", [P, NT, D], F32)
        acc = sb("acc", [P, NT, D], F32)
        x2T = sb("x2T", [P, NT * P], F32)
        x2h = sb("x2h", [P, 2, NT * P], F16)
        zeros = sb("zeros", [P, 256], F16)
        ident = sb("ident", [P, P], F32)
        ident16 = sb("ident16", [P, P], F16)
        b1_rows = sb("b1_rows", [NE * HC, P], F32)
        b1T = sb("b1T", [P, NE * HC], F32)
        b2_rows = sb("b2_rows", [NE, D], F32)
        gw = sb("gw", [P, E], F32)
        gb = sb("gb", [P, E], F32)
        bo_sb = sb("bo_sb", [P, D], F32)
        gates = sb("gates", [P, 4], F32)
        scales = sb("scales", [P, 2], F32)
        nmax = sb("nmax", [P, NH, QT], F32)
        shift16 = sb("shift16", [P, NH, QT], F16)
        rsum = sb("rsum", [P, NH, QT], F32)
        stats = sb("stats", [P, 2 * NT, 6], F32)
        mv = sb("mv", [P, 2 * NT, 2], F32)
        vare = sb("vare", [P, 2 * NT], F32)
        rstd = sb("rstd", [P, 2 * NT], F32)
        c_mhalf = sb("c_mhalf", [P, 2 * NT], F32)
        c_sw = sb("c_sw", [P, 1], F32)
        c_e = sb("c_e", [P, QT], F32)
        logit = sb("logit", [P, NT, 2 * E], F32)
        top8 = sb("top8", [P, NT, 8], F32)
        pick8 = sb("pick8", [P, NT, 8], F32)
        marked = sb("marked", [P, NT, 2 * E], F32)
        mask = sb("mask", [P, NT, E], F32)
        first = sb("first", [P, NT, E], F32)
        gdiff = sb("gdiff", [P, NT], F32)
        gexp = sb("gexp", [P, NT], F32)
        gsum = sb("gsum", [P, NT], F32)
        gtop = sb("gtop", [P, NT, 2], F32)
        comb = sb("comb", [P, NT, NE], F32)
        comb_s = sb("comb_s", [P, NT, NE], F32)
        combT = cT[0:NE, 0, :].bitcast(F32)

        banks = stack.enter_context(nc.psum_tensor("banks", [P, 8, 512], F32))

        def span(first, n):
            return banks[:, first:first + 2, :].rearrange("p a n -> p (a n)")[:, 0:n]

        o_ps = banks[:, 6, 0:QT * (DH + 1)].rearrange("p (q d) -> p q d", q=QT)
        misc = banks[:, 7, :]

        ld_x, ld_small, ld_rows = sem("ld_x"), sem("ld_small"), sem("ld_rows")
        ld_ctx = [sem(f"ld_ctx{b}") for b in range(B)]
        wp_hi, wp_scaled, wp_lo = sem("wp_hi"), sem("wp_scaled"), sem("wp_lo")
        ld_w = [sem(f"ld_w{w}") for w in range(NW)]
        ld_f = [sem(f"ld_f{j}") for j in range(NE)]
        zeros_ready = sem("zeros_ready")
        consts = sem("consts")
        pool_chain = sem("pool_chain")
        dve_chain = sem("dve_chain")
        var_ready = sem("var_ready")
        rstd_ready = sem("rstd_ready")
        xn_ready = sem("xn_ready")
        tanh_done = sem("tanh_done")
        xb_done = sem("xb_done")
        w_hi, w_lo = sem("w_hi"), sem("w_lo")
        item_ps = sem("item_ps")
        item_hi, item_lo = sem("item_hi"), sem("item_lo")
        k_st = [sem(f"k_st{n}") for n in range(B * PAIRS)]
        q_st = [sem(f"q_st{n}") for n in range(PAIRS)]
        max_ps = sem("max_ps")
        max_done = sem("max_done")
        shift_ready = sem("shift_ready")
        shift_done = sem("shift_done")
        score_ps = sem("score_ps")
        exp_done = sem("exp_done")
        ph_act, ph_dve = sem("ph_act"), sem("ph_dve")
        pl_done = sem("pl_done")
        pd_done = sem("pd_done")
        pv_ps = sem("pv_ps")
        o_done = sem("o_done")
        misc_ps = sem("misc_ps")
        misc_hi = sem("misc_hi")
        misc_done = sem("misc_done")
        gexp_go, gexp_done = sem("gexp_go"), sem("gexp_done")
        comb_ready = sem("comb_ready")
        e_scaled, e_hi, e_lo = sem("e_scaled"), sem("e_hi"), sem("e_lo")
        f_hi, f_lo = sem("f_hi"), sem("f_lo")
        h_ps = sem("h_ps")
        gelu_done = sem("gelu_done")
        hh_done, hl_done = sem("hh_done"), sem("hl_done")
        hd_done = sem("hd_done")
        y_ps = sem("y_ps")
        y_done = sem("y_done")
        stored = sem("stored")

        x_d = x.rearrange("b (t p) d -> p (b t) d", p=P)
        ctx_d = ctx_in.rearrange("b (t p) d -> b p t d", p=P)
        out_d = out.rearrange("b (t p) d -> b p t d", p=P)
        w_d = {WK2: Wk2, WK1: Wk1, WQ: Wq1, WV2: Wv2, WV1: Wv1}

        def ring_a(w):
            n = SPLIT_ORDER.index(w)
            return ring[:, n // 2, n % 2, :]

        def ring_f(j):
            return ring[:, (3 + j) % RING]

        def wait_split(engine, w):
            if w in BY_POOL:
                engine.wait_ge(wp_lo, BY_POOL.index(w) + 1)
            else:
                engine.wait_ge(w_lo, SPLIT_AT[w])

        def ctx_cols(b, t):
            return slice(b * T2 + t * P, b * T2 + (t + 1) * P)

        def item_out(n):
            kind = ITEMS[n][0]
            return span(2 * SLOT[n], KEYS if kind == "k" else 512)

        block = stack.enter_context(nc.Block())

        @block.sync
        def _(sp):
            def load_a(w):
                dst = ring_a(w)
                if w == WO:
                    sp.dma_start(dst.rearrange("p (c n) -> p c n", n=D),
                                 Wo.rearrange("(c p) n -> p c n", p=P)).then_inc(ld_w[w], 16)
                else:
                    sp.dma_start(dst, w_d[w]).then_inc(ld_w[w], 16)

            def load_f(j):
                e = EORDER[j]
                slot = ring_f(j)
                src1, src2 = (ws1, ws2) if e == E else (w1[e], w2[e])
                if 1 <= j < RING:
                    for w in SPLIT_ORDER[:2 * j]:
                        wait_split(sp, w)
                elif RING <= j < RING + EARLY:
                    sp.wait_ge(e_lo, j - RING + 1)
                elif j >= RING + EARLY:
                    sp.wait_ge(f_lo, j - RING - EARLY + 1)
                sp.dma_start(slot[:, 0, :], src1).then_inc(ld_f[j], 16)
                sp.dma_start(slot[:, 1, :].rearrange("p (c n) -> p c n", n=D),
                             src2.rearrange("(c p) n -> p c n", p=P)).then_inc(ld_f[j], 16)

            sp.dma_start(x_sb[:, :, :], x_d).then_inc(ld_x, 16)
            sp.dma_start(ctx_sb[:, 0:T2 // P, :], ctx_d[0]).then_inc(ld_ctx[0], 16)
            for w in (WK2, WK1, WQ):
                load_a(w)
            sp.dma_start(gates[:, 0:1], g_xattn.partition_broadcast(P)).then_inc(ld_small, 16)
            sp.dma_start(gates[:, 1:2], g_ffn.partition_broadcast(P)).then_inc(ld_small, 16)
            sp.dma_start(ctx_sb[:, T2 // P:, :], ctx_d[1]).then_inc(ld_ctx[1], 16)
            for w in (WV2, WV1, WO):
                load_a(w)
            sp.dma_start(bo_sb[:, :], bo.partition_broadcast(P)).then_inc(ld_small, 16)

            def stack_k(b, p0, p1):
                done = k_st[b * PAIRS + p0]
                n = p1 - p0
                sp.wait_ge(item_lo, ITEMS.index(("k", b, p1 - 1)) + 1)
                if b > 0:
                    sp.wait_ge(score_ps, 2 * 2 * p1)
                for half in range(2):
                    src = slice(DH * half, DH * half + DH)
                    heads = slice(place(2 * p0 + half), place(2 * p1 + half - 2) + 1)
                    sp.dma_start(kab[0:DH, :, heads, :],
                                 k_nat[src, 0:1, p0:p1, :].broadcast_to([DH, 2, p1 - p0, KEYS])).then_inc(done, 16)
                    sp.dma_start(kab[DH:P, 0, heads, :], k_nat[src, 1, p0:p1, :]).then_inc(done, 16)

            def stack_q(p0, p1):
                done = q_st[p0]
                sp.wait_ge(item_lo, ITEMS.index(("q", p1 - 1)) + 1)
                for half in range(2):
                    src = slice(DH * half, DH * half + DH)
                    heads = slice(place(2 * p0 + half), place(2 * p1 + half - 2) + 1)
                    sp.dma_start(qab[0:DH, :, heads, :], q_nat[src, :, p0:p1, :]).then_inc(done, 16)
                    sp.dma_start(qab[DH:P, 0, heads, :], q_nat[src, 0, p0:p1, :]).then_inc(done, 16)

            load_f(0)
            sp.dma_start(gb[:, :], gate_b.partition_broadcast(P)).then_inc(ld_rows, 16)
            sp.dma_start(gw[:, :], gate_w).then_inc(ld_rows, 16)
            sp.dma_start(b1_rows[0:E * HC, :], b1.rearrange("e (c p) -> (e c) p", p=P)).then_inc(ld_rows, 16)
            sp.dma_start(b1_rows[E * HC:, :], bs1.rearrange("(c p) -> c p", p=P)).then_inc(ld_rows, 16)
            sp.dma_start(b2_rows[0:E, :], b2).then_inc(ld_rows, 16)
            sp.dma_start(b2_rows[E:, :], bs2.rearrange("(a n) -> a n", a=1)).then_inc(ld_rows, 16)
            for n, (p0, p1) in enumerate(GROUPS[0]):
                stack_k(0, p0, p1)
                stack_q(p0, p1)
                load_f(1 + n)
            for j in range(1 + len(GROUPS[0]), RING):
                load_f(j)
            for p0, p1 in GROUPS[1]:
                stack_k(1, p0, p1)
            for j in range(RING, NE):
                load_f(j)
            for b in range(B):
                sp.wait_ge(y_done, QT * NE * (b + 1))
                sp.dma_start(out_d[b], acc[:, QT * b:QT * b + QT, :]).then_inc(stored, 16)
            sp.wait_ge(stored, 16 * B)

        @block.gpsimd
        def _(pool):
            n = 0

            def link(ins):
                nonlocal n
                n += 1
                ins.then_inc(pool_chain, 1)
                pool.wait_ge(pool_chain, n)

            nc.gpsimd.memset(c_mhalf[:, :], -0.5).then_inc(consts, 1)
            link(nc.gpsimd.memset(ident[:, :], 0.0))
            nc.gpsimd.affine_select(out=ident[:, :], in_=ident[:, :], compare_op=ALU.not_equal, fill=1.0,
                                    base=0, pattern=[[-1, P]], channel_multiplier=1).then_inc(consts, 1)
            link(nc.gpsimd.memset(ident16[:, :], 0.0))
            nc.gpsimd.affine_select(out=ident16[:, :], in_=ident16[:, :], compare_op=ALU.not_equal, fill=1.0,
                                    base=0, pattern=[[-1, P]], channel_multiplier=1).then_inc(consts, 1)
            pool.wait_ge(consts, 3)
            nc.gpsimd.memset(k_b[DH:DH + 1, :, :].bitcast(F32), SHIFT_PAIR).then_inc(consts, 1)
            pool.wait_ge(consts, 4)
            pool.wait_ge(var_ready, 1)
            nc.gpsimd.tensor_tensor(rstd[:, 0:NT], vare[:, 0:NT], c_mhalf[:, 0:NT], ALU.pow).then_inc(rstd_ready, 1)
            pool.wait_ge(rstd_ready, 1)
            nc.gpsimd.memset(v_hi[:, :, :, DH:DH + 1], S_ACTV).then_inc(consts, 1)
            link(nc.gpsimd.memset(c_sw[:, :], S_W))
            link(nc.gpsimd.memset(c_e[:, :], 2.718281828459045))
            nc.gpsimd.memset(logit[:, :, :], NONE).then_inc(consts, 1)
            nc.gpsimd.memset(pick8[:, :, :], NONE).then_inc(consts, 1)
            nc.gpsimd.memset(comb[:, :, :], 1.0).then_inc(consts, 1)

            def split_early(j):
                pool.wait_ge(ld_f[j], 32)
                src = ring_f(j).rearrange("p a n -> p (a n)")
                hi = wf[:, 0, EORDER[j], :, :].rearrange("p a n -> p (a n)")
                s_w = c_sw[:, :].broadcast_to([P, 2 * 512])
                nc.gpsimd.tensor_tensor(hi, src, s_w, ALU.mult).then_inc(e_hi, 1)
                pool.wait_ge(e_hi, j + 1)
                nc.gpsimd.tensor_tensor(src, src, s_w, ALU.mult).then_inc(e_scaled, 1)
                pool.wait_ge(e_scaled, j + 1)
                nc.gpsimd.tensor_tensor(wf[:, 1, EORDER[j], :, :].rearrange("p a n -> p (a n)"), src, hi,
                                        ALU.subtract).then_inc(e_lo, 1)

            def split_by_pool(w):
                n = BY_POOL.index(w)
                s_w = c_sw[:, :].broadcast_to([P, 512])
                pool.wait_ge(ld_w[w], 16)
                nc.gpsimd.tensor_tensor(wa[:, 0, w, :], ring_a(w), s_w, ALU.mult).then_inc(wp_hi, 1)
                pool.wait_ge(wp_hi, n + 1)
                nc.gpsimd.tensor_tensor(ring_a(w), ring_a(w), s_w, ALU.mult).then_inc(wp_scaled, 1)
                pool.wait_ge(wp_scaled, n + 1)
                nc.gpsimd.tensor_tensor(wa[:, 1, w, :], ring_a(w), wa[:, 0, w, :], ALU.subtract).then_inc(wp_lo, 1)

            split_by_pool(WV2)
            split_early(0)
            pool.wait_ge(tanh_done, 1)
            pool.wait_ge(ld_small, 48)
            link(nc.gpsimd.tensor_scalar(bo_sb[:, :], bo_sb[:, :], gates[:, 2:3], None, ALU.mult))
            pool.wait_ge(xn_ready, NT)
            for t in range(NT):
                nc.gpsimd.tensor_tensor(x_sb[:, t, :], x_sb[:, t, :], bo_sb[:, :], ALU.add).then_inc(xb_done, 1)

            def prob_lo(j, g):
                if g == 0:
                    pool.wait_ge(ph_act, j + 1)
                else:
                    pool.wait_ge(ph_dve, j + 1)
                n = lo_tiles(j) if g else 3
                dst = slice(3 * g, 3 * g + n)
                nc.gpsimd.tensor_tensor(p_lo[:, j % 3, dst, :].rearrange("p t n -> p (t n)"),
                                        prob[:, j % 2, g, 0:n * T1],
                                        p_hi[:, j % 3, dst, :].rearrange("p t n -> p (t n)"),
                                        ALU.subtract).then_inc(pl_done, 1)

            for j in range(1, EARLY):
                if j == EARLY - 1:
                    split_by_pool(WO)
                split_early(j)

            for i in range(STEPS):
                if 0 <= i - HI_LAG < NH:
                    prob_lo(i - HI_LAG, 0)
                    if lo_tiles(i - HI_LAG) > 0:
                        prob_lo(i - HI_LAG, 1)
                for b, s in tail_of(i - 1):
                    if s == TAIL_WO:
                        t = NT + QT * b
                        pool.wait_ge(var_ready, 2 + b)
                        nc.gpsimd.tensor_tensor(rstd[:, t:t + QT], vare[:, t:t + QT], c_mhalf[:, t:t + QT],
                                                ALU.pow).then_inc(rstd_ready, 1)
                    if s == TAIL_GATE:
                        pool.wait_ge(gexp_go, b + 1)
                        nc.gpsimd.tensor_tensor(gexp[:, QT * b:QT * b + QT], c_e[:, :],
                                                gdiff[:, QT * b:QT * b + QT], ALU.pow).then_inc(gexp_done, 1)
                k = i - FFN0 - 1
                if 0 <= k < NF:
                    pool.wait_ge(hh_done, hi_count(k) + 1)
                    c0, c1 = hid_parts(k)[0]
                    cols = slice(c0 * T1, c1 * T1)
                    nc.gpsimd.tensor_tensor(hid_lo[:, k % HB, cols], hid[:, k % 2, cols], hid_hi[:, k % HB, cols],
                                            ALU.subtract).then_inc(hl_done, 1)

        @block.scalar
        def _(act):
            def split_a(w):
                act.wait_ge(ld_w[w], 16)
                nc.scalar.activation(wa[:, 0, w, :], ring_a(w), ACT.Copy, scale=S_W).then_inc(w_hi, 1)

            def tanh_gates():
                act.wait_ge(ld_small, 48)
                nc.scalar.activation(gates[:, 2:4], gates[:, 0:2], ACT.Tanh).then_inc(tanh_done, 1)

            def item_of(n):
                item = ITEMS[n]
                for w in SPLIT_BEFORE.get(n, []):
                    if w not in BY_POOL:
                        split_a(w)
                if n == 8:
                    tanh_gates()
                act.wait_ge(item_ps, n + 1)
                src = item_out(n)
                kind = item[0]
                if kind == "tx":
                    dst, s = xT[:, 0, :], S_ACTV
                elif kind == "tc":
                    dst, s = cT[:, 0, item[1] * T2:(item[1] + 1) * T2], S_ACTV
                elif kind == "k":
                    _, b, p = item
                    if b > 0:
                        act.wait_ge(k_st[group_of(0, p)], 64)
                    dst, s = k_nat[:, 0, p, :], 1.0 / S_W
                elif kind == "q":
                    dst, s = q_nat[:, 0, item[1], :], 1.0 / S_W
                else:
                    _, b, t = item
                    dst, s = v_hi[:, b * KT + t, :, 0:DH], 1.0 / S_W
                    src = src.rearrange("p (h d) -> p h d", d=DH)
                nc.scalar.activation(dst, src, ACT.Copy, scale=s).then_inc(item_hi, 1)

            for n in range(NI - LATE):
                item_of(n)

            def shift_out(j):
                act.wait_ge(misc_ps, MISC[("shift", j)] + 1)
                b, h = divmod(j, HEADS)
                nc.scalar.activation(q_b[DH:DH + 1, place(h), b * T1:(b + 1) * T1], misc[DH:DH + 1, 0:T1],
                                     ACT.Copy).then_inc(shift_done, 1)

            def exp_half(j, g):
                act.wait_ge(score_ps, 2 * j + g + 1)
                if j >= 2:
                    act.wait_ge(pl_done, pool_lo(j - 2, g))
                    if g == 1:
                        act.wait_ge(pd_done, j - 1)
                nc.scalar.activation(prob[:, j % 2, g, :], span(2 + 2 * g, 3 * T1), ACT.Exp,
                                     scale=DH ** -0.5 / S_SCORE).then_inc(exp_done, 1)

            for i in range(STEPS):
                for n in late_items(i, 0):
                    item_of(n)
                if i == 1:
                    shift_out(0)
                if i < ST_LAG:
                    for n in late_items(i, 1):
                        item_of(n)
                for b, s in tail_of(i - 1):
                    if s in (TAIL_O0, TAIL_O1):
                        act.wait_ge(misc_ps, MISC[(s, b)] + 1)
                        t = QT * b + s
                        nc.scalar.activation(oT[:, 0, t, :], misc, ACT.Copy, scale=S_ACTV).then_inc(misc_hi, 1)
                    if s == TAIL_X:
                        act.wait_ge(misc_ps, MISC[(s, b)] + 1)
                        nc.scalar.activation(x2h[:, 0, b * T1:(b + 1) * T1], misc[:, 0:T1], ACT.Copy,
                                             scale=S_ACTV).then_inc(misc_hi, 1)
                j = i - ST_LAG
                if 0 <= j < NH:
                    exp_half(j, 0)
                    act.wait_ge(exp_done, 2 * j + 1)
                    if j >= 3:
                        act.wait_ge(pv_ps, QT * (j - 2))
                    nc.scalar.activation(p_hi[:, j % 3, 0:3, :].rearrange("p t n -> p (t n)"), prob[:, j % 2, 0, :],
                                         ACT.Copy).then_inc(ph_act, 1)
                if 2 <= i <= NH:
                    shift_out(i - 1)
                    for n in late_items(i, 1):
                        item_of(n)
                if 0 <= j < NH:
                    exp_half(j, 1)
                k = i - FFN0
                if 0 <= k < NF:
                    e = EORDER[k % NE]
                    if k >= 2:
                        act.wait_ge(hl_done, k - 1)
                        if shared(k - 1) > 0:
                            act.wait_ge(hd_done, shared(k - 1))
                    for c in range(HC):
                        act.wait_ge(h_ps, HC // 2 * k + c // 2 + 1)
                        nc.scalar.activation(hid[:, k % 2, c * T1:(c + 1) * T1],
                                             span(2 * (k % 2), HC * T1)[:, c * T1:(c + 1) * T1], ACT.Gelu,
                                             bias=b1T[:, e * HC + c:e * HC + c + 1],
                                             scale=1.0 / (S_ACTV * S_W)).then_inc(gelu_done, 1)
                j = i - FSPLIT0
                if EARLY <= j < NE:
                    act.wait_ge(ld_f[j], 32)
                    nc.scalar.activation(wf[:, 0, EORDER[j], :, :], ring_f(j), ACT.Copy, scale=S_W).then_inc(f_hi, 1)

        @block.vector
        def _(dve):
            n_chain = 0
            n_mhi = 0

            def mark(ins):
                nonlocal n_chain
                n_chain += 1
                ins.then_inc(dve_chain, 1)

            def settle():
                dve.wait_ge(dve_chain, n_chain)

            def link(ins):
                mark(ins)
                settle()

            def row_statistics(src, first, tiles):
                for t in range(tiles):
                    mark(nc.vector.bn_stats(stats[:, first + t, :], src[:, t, :]))
                settle()
                for t in range(tiles):
                    mark(nc.vector.bn_aggr(mv[:, first + t, :], stats[:, first + t, :]))
                settle()
                nc.vector.tensor_scalar(vare[:, first:first + tiles], mv[:, first:first + tiles, 1], EPS, None,
                                        ALU.add).then_inc(var_ready, 1)

            def normalise_rows(src, first, tiles, phase):
                dve.wait_ge(rstd_ready, phase)
                for t in range(tiles):
                    nc.vector.tensor_scalar(xn[:, (first + t) % NT, :], src[:, t, :], mv[:, first + t, 0:1],
                                            rstd[:, first + t:first + t + 1], ALU.subtract,
                                            ALU.mult).then_inc(xn_ready, 1)

            def split_a(w):
                dve.wait_ge(w_hi, SPLIT_AT[w])
                nc.vector.scalar_tensor_tensor(out=wa[:, 1, w, :], in0=ring_a(w), scalar=S_W, in1=wa[:, 0, w, :],
                                               op0=ALU.mult, op1=ALU.subtract).then_inc(w_lo, 1)

            def item_of(n):
                item = ITEMS[n]
                if item[0] == "tx":
                    normalise_rows(x_sb, 0, NT, 1)
                for w in SPLIT_BEFORE.get(n, []):
                    if w not in BY_POOL:
                        split_a(w)
                dve.wait_ge(item_hi, n + 1)
                src = item_out(n)
                kind = item[0]
                if kind == "tx":
                    dst, hi, s = xT[:, 1, :], xT[:, 0, :], S_ACTV
                elif kind == "tc":
                    cols = slice(item[1] * T2, (item[1] + 1) * T2)
                    dst, hi, s = cT[:, 1, cols], cT[:, 0, cols], S_ACTV
                elif kind == "k":
                    p = item[2]
                    dst, hi, s = k_nat[:, 1, p, :], k_nat[:, 0, p, :], 1.0 / S_W
                elif kind == "q":
                    p = item[1]
                    dst, hi, s = q_nat[:, 1, p, :], q_nat[:, 0, p, :], 1.0 / S_W
                else:
                    t = item[1] * KT + item[2]
                    dst, hi, s = v_lo[:, t, :, :], v_hi[:, t, :, 0:DH], 1.0 / S_W
                    src = src.rearrange("p (h d) -> p h d", d=DH)
                nc.vector.scalar_tensor_tensor(out=dst, in0=src, scalar=s, in1=hi, op0=ALU.mult,
                                               op1=ALU.subtract).then_inc(item_lo, 1)

            nc.vector.memset(zeros[:, :], 0.0).then_inc(zeros_ready, 1)
            dve.wait_ge(ld_x, 16)
            row_statistics(x_sb, 0, NT)
            for n in range(NI - LATE):
                item_of(n)

            dve.wait_ge(tanh_done, 1)
            mark(nc.vector.tensor_scalar(scales[:, 0:1], gates[:, 2:3], 1.0 / (S_ACTV * S_W), None, ALU.mult))
            mark(nc.vector.tensor_scalar(scales[:, 1:2], gates[:, 3:4], 1.0 / S_W, None, ALU.mult))

            def take_max(i, q):
                dve.wait_ge(max_ps, QT * i + q + 1)
                nc.vector.tensor_reduce(nmax[:, i, q:q + 1], span(0, KEYS), AX_X, ALU.max,
                                        negate=True).then_inc(max_done, 1)

            def reciprocals(j):
                dve.wait_ge(pv_ps, QT * (j + 1))
                mark(nc.vector.reciprocal(rsum[:, j, :], o_ps[:, :, DH]))

            def normalise(j):
                b, h = divmod(j, HEADS)
                settle()
                nc.vector.tensor_tensor(o_sb[:, QT * b:QT * b + QT, h * DH:(h + 1) * DH], o_ps[:, :, 0:DH],
                                        rsum[:, j, :].unsqueeze(2).broadcast_to([P, QT, DH]),
                                        ALU.mult).then_inc(o_done, 1)

            def lo_of_misc(dst, hi, n):
                nc.vector.scalar_tensor_tensor(out=dst, in0=misc[:, 0:n], scalar=S_ACTV, in1=hi, op0=ALU.mult,
                                               op1=ALU.subtract).then_inc(misc_done, 1)

            def tail_first(b, s):
                tiles = slice(QT * b, QT * b + QT)
                if s == TAIL_X:
                    normalise_rows(acc[:, tiles, :], NT + QT * b, QT, 2 + b)
                if s == TAIL_COMB:
                    dve.wait_ge(gexp_done, b + 1)
                    link(nc.vector.tensor_scalar(gsum[:, tiles], gexp[:, tiles], 1.0, None, ALU.add))
                    link(nc.vector.reciprocal(gtop[:, tiles, 0], gsum[:, tiles]))
                    mark(nc.vector.tensor_tensor(gtop[:, tiles, 1], gtop[:, tiles, 0], gexp[:, tiles], ALU.mult))
                    link(nc.vector.tensor_tensor(first[:, tiles, :], first[:, tiles, :],
                                                 gtop[:, tiles, 0:1].broadcast_to([P, QT, E]), ALU.mult))
                    link(nc.vector.tensor_tensor(first[:, tiles, :], first[:, tiles, :],
                                                 gtop[:, tiles, 1:2].broadcast_to([P, QT, E]), ALU.max))
                    link(nc.vector.tensor_tensor(comb[:, tiles, 0:E], first[:, tiles, :], mask[:, tiles, :],
                                                 ALU.mult))
                    nc.vector.tensor_scalar(comb_s[:, tiles, :], comb[:, tiles, :], scales[:, 1:2], None,
                                            ALU.mult).then_inc(comb_ready, 1)
                    dve.wait_ge(comb_ready, b + 1)

            def tail(b, s):
                nonlocal n_mhi
                tiles = slice(QT * b, QT * b + QT)
                cols = slice(b * T1, (b + 1) * T1)
                dve.wait_ge(misc_ps, MISC[(s, b)] + 1)
                if s in (TAIL_O0, TAIL_O1, TAIL_X):
                    n_mhi += 1
                    dve.wait_ge(misc_hi, n_mhi)
                if s in (TAIL_O0, TAIL_O1):
                    t = QT * b + s
                    lo_of_misc(oT[:, 1, t, :], oT[:, 0, t, :], INNER)
                elif s == TAIL_WO:
                    dve.wait_ge(xb_done, NT)
                    nc.vector.scalar_tensor_tensor(
                        out=acc[:, tiles, :].rearrange("p t d -> p (t d)"), in0=misc[:, 0:QT * D],
                        scalar=scales[:, 0:1], in1=x_sb[:, tiles, :].rearrange("p t d -> p (t d)"),
                        op0=ALU.mult, op1=ALU.add).then_inc(misc_done, 1)
                    dve.wait_ge(misc_done, MISC[(s, b)] + 1 - shifts_before(MISC[(s, b)]))
                    row_statistics(acc[:, tiles, :], NT + QT * b, QT)
                elif s == TAIL_X:
                    link(nc.vector.tensor_copy(x2T[:, cols], misc[:, 0:T1]))
                    lo_of_misc(x2h[:, 1, cols], x2h[:, 0, cols], T1)
                elif s == TAIL_GATE:
                    nc.vector.tensor_tensor(logit[:, tiles, 0:E], misc[:, 0:QT * E].rearrange("p (t e) -> p t e", e=E),
                                            gb[:, :].unsqueeze(1).broadcast_to([P, QT, E]),
                                            ALU.add).then_inc(misc_done, 1)
                    dve.wait_ge(misc_done, MISC[(s, b)] + 1 - shifts_before(MISC[(s, b)]))
                    for t in range(QT * b, QT * b + QT):
                        mark(nc.vector.max(top8[:, t, :], logit[:, t, 0:E]))
                    settle()
                    mark(nc.vector.tensor_copy(pick8[:, tiles, 0:2], top8[:, tiles, 0:2]))
                    nc.vector.tensor_tensor(gdiff[:, tiles], top8[:, tiles, 1], top8[:, tiles, 0],
                                            ALU.subtract).then_inc(gexp_go, 1)
                    mark(nc.vector.tensor_tensor(first[:, tiles, :], logit[:, tiles, 0:E],
                                                 top8[:, tiles, 0:1].broadcast_to([P, QT, E]), ALU.is_equal))
                    settle()
                    for t in range(QT * b, QT * b + QT):
                        mark(nc.vector.match_replace(marked[:, t, :], pick8[:, t, :], logit[:, t, :], PICKED))
                    settle()
                    mark(nc.vector.tensor_scalar(mask[:, tiles, :], marked[:, tiles, 0:E], PICKED, None,
                                                 ALU.is_equal))
                elif s == TAIL_COMB:
                    nc.vector.tensor_copy(combT[:, cols], misc[0:NE, 0:T1]).then_inc(misc_done, 1)
                elif s == TAIL_B2:
                    nc.vector.scalar_tensor_tensor(
                        out=acc[:, tiles, :].rearrange("p t d -> p (t d)"), in0=misc[:, 0:QT * D],
                        scalar=gates[:, 3:4], in1=acc[:, tiles, :].rearrange("p t d -> p (t d)"),
                        op0=ALU.mult, op1=ALU.add).then_inc(misc_done, 1)
                    dve.wait_ge(misc_done, MISC[(s, b)] + 1 - shifts_before(MISC[(s, b)]))

            def second_hi(j):
                dve.wait_ge(exp_done, 2 * j + 2)
                if j >= 3:
                    dve.wait_ge(pv_ps, QT * (j - 2))
                nc.vector.tensor_copy(p_hi[:, j % 3, 3:6, :].rearrange("p t n -> p (t n)"),
                                      prob[:, j % 2, 1, :]).then_inc(ph_dve, 1)

            def last_lo(j):
                dve.wait_ge(ph_dve, j + 1)
                n = lo_tiles(j)
                nc.vector.tensor_tensor(p_lo[:, j % 3, 3 + n:6, :].rearrange("p t n -> p (t n)"),
                                        prob[:, j % 2, 1, n * T1:],
                                        p_hi[:, j % 3, 3 + n:6, :].rearrange("p t n -> p (t n)"),
                                        ALU.subtract).then_inc(pd_done, 1)

            for i in range(STEPS):
                k = i - FFN0 - 1
                if 0 <= k < NF:
                    if k >= HB:
                        dve.wait_ge(y_ps, k - HB + 1)
                    for c0, c1 in hid_parts(k):
                        dve.wait_ge(gelu_done, HC * k + c1)
                        cols = slice(c0 * T1, c1 * T1)
                        nc.vector.tensor_copy(hid_hi[:, k % HB, cols], hid[:, k % 2, cols]).then_inc(hh_done, 1)
                    if k in SHARED_LO:
                        dve.wait_ge(hh_done, hi_count(k + 1))
                        nc.vector.tensor_tensor(hid_lo[:, k % HB, cols], hid[:, k % 2, cols],
                                                hid_hi[:, k % HB, cols], ALU.subtract).then_inc(hd_done, 1)
                if i < NH:
                    take_max(i, 0)
                for n in late_items(i, 0):
                    item_of(n)
                for b, s in tail_of(i - 1):
                    tail(b, s)
                for b, s in tail_of(i):
                    tail_first(b, s)
                if 0 <= i - HI_LAG < NH:
                    second_hi(i - HI_LAG)
                if i < NH:
                    take_max(i, 1)
                if 0 <= i - HI_LAG < NH:
                    last_lo(i - HI_LAG)
                if 0 <= i - PV_LAG < NH:
                    reciprocals(i - PV_LAG)
                if i < NH:
                    dve.wait_ge(max_done, QT * (i + 1))
                    nc.vector.tensor_scalar(shift16[:, i, :], nmax[:, i, :], 1.0 / SHIFT_ROW, SHIFT_P, ALU.mult,
                                            ALU.add).then_inc(shift_ready, 1)
                if 0 <= i - PV_LAG < NH:
                    normalise(i - PV_LAG)
                for n in late_items(i, 1):
                    item_of(n)
                k = i - FFN0 - 3
                if 0 <= k < NF:
                    b, e = k // NE, EORDER[k % NE]
                    dve.wait_ge(y_ps, k + 1)
                    for t in range(QT):
                        if k >= 1:
                            dve.wait_ge(y_done, QT * (k - 1) + t + 1)
                        nc.vector.scalar_tensor_tensor(
                            out=acc[:, QT * b + t, :], in0=banks[:, 4 + k % 2, t * D:(t + 1) * D],
                            scalar=comb_s[:, QT * b + t, e:e + 1], in1=acc[:, QT * b + t, :],
                            op0=ALU.mult, op1=ALU.add).then_inc(y_done, 1)
                j = i - FSPLIT0 - 1
                if EARLY <= j < NE:
                    dve.wait_ge(f_hi, j - EARLY + 1)
                    e = EORDER[j]
                    nc.vector.scalar_tensor_tensor(
                        out=wf[:, 1, e, :, :].rearrange("p a n -> p (a n)"),
                        in0=ring_f(j).rearrange("p a n -> p (a n)"), scalar=S_W,
                        in1=wf[:, 0, e, :, :].rearrange("p a n -> p (a n)"),
                        op0=ALU.mult, op1=ALU.subtract).then_inc(f_lo, 1)
                if i == BIAS_STEP:
                    dve.wait_ge(misc_ps, MISC[("b1", 0)] + 1)
                    nc.vector.tensor_copy(b1T[:, :], misc[:, 0:NE * HC]).then_inc(misc_done, 1)

        @block.tensor
        def _(pe):
            def three(dst, w, a, start=True, stop=True):
                nc.tensor.matmul(dst, w[0], a[0], start=start, stop=False)
                nc.tensor.matmul(dst, w[0], a[1], start=False, stop=False)
                return nc.tensor.matmul(dst, w[1], a[0], start=False, stop=stop)

            def w_pair(w, cols):
                return wa[:, 0, w, cols], wa[:, 1, w, cols]

            def x_pair(cols):
                return xT[:, 0, cols], xT[:, 1, cols]

            def c_pair(cols):
                return cT[:, 0, cols], cT[:, 1, cols]

            def keep_warm(n, bank):
                for _ in range(n):
                    nc.tensor.matmul(banks[:, bank, 0:256], zeros[:, 0:P], zeros[:, :],
                                     start=True, stop=True)

            pe.wait_ge(zeros_ready, 1)
            keep_warm(WARM_START, 2 * SLOT[3])
            pe.wait_ge(consts, 3)
            def read_out(n):
                if n > 0:
                    pe.wait_ge(item_lo, n)

            def item_of(n):
                item = ITEMS[n]
                kind = item[0]
                dst = item_out(n)
                read_out(before(n, SLOT[n]))
                if kind == "tx":
                    keep_warm(WARM_LAYERNORM, 2 * SLOT[3])
                    for t in range(NT):
                        pe.wait_ge(xn_ready, t + 1)
                        last = nc.tensor.transpose(dst[:, t * P:(t + 1) * P], xn[:, t, :], ident[:, :])
                elif kind == "tc":
                    b = item[1]
                    pe.wait_ge(ld_ctx[b], 16)
                    for t in range(T2 // P):
                        last = nc.tensor.transpose(dst[:, t * P:(t + 1) * P], ctx_sb[:, b * (T2 // P) + t, :],
                                                   ident[:, :])
                elif kind == "k":
                    _, b, p = item
                    pair = slice(p * P, (p + 1) * P)
                    wait_split(pe, WK2)
                    pe.wait_ge(item_lo, ITEMS.index(("tc", b)) + 1)
                    three(dst[:, 0:T2], w_pair(WK2, pair), c_pair(slice(b * T2, (b + 1) * T2)))
                    wait_split(pe, WK1)
                    pe.wait_ge(item_lo, ITEMS.index(("tx", 0)) + 1)
                    last = three(dst[:, T2:KEYS], w_pair(WK1, pair), x_pair(slice(b * T1, (b + 1) * T1)))
                elif kind == "q":
                    p = item[1]
                    wait_split(pe, WQ)
                    last = three(dst, w_pair(WQ, slice(p * P, (p + 1) * P)), x_pair(slice(0, B * T1)))
                else:
                    _, b, t = item
                    if t < T2 // P:
                        wait_split(pe, WV2)
                        pe.wait_ge(item_lo, ITEMS.index(("tc", b)) + 1)
                        last = three(dst, c_pair(ctx_cols(b, t)), w_pair(WV2, slice(0, INNER)))
                    else:
                        wait_split(pe, WV1)
                        at = b * T1 + (t - T2 // P) * P
                        last = three(dst, x_pair(slice(at, at + P)), w_pair(WV1, slice(0, INNER)))
                last.then_inc(item_ps, 1)

            for n in range(NI - LATE):
                item_of(n)

            def max_scores(i, q):
                b, h = divmod(i, HEADS)
                if q == 0:
                    pe.wait_ge(k_st[b * PAIRS + group_of(b, h // 2)], 64)
                    pe.wait_ge(q_st[group_of(0, h // 2)], 64)
                if i + q > 0:
                    pe.wait_ge(max_done, QT * i + q)
                h = place(h)
                queries = q_a[0:DH, h, b * T1 + q * P:b * T1 + (q + 1) * P]
                nc.tensor.matmul(span(0, KEYS)[:, 0:T2], queries, k_a[0:DH, h, 0:T2], start=True, stop=True)
                nc.tensor.matmul(span(0, KEYS)[:, T2:KEYS], queries, k_a[0:DH, h, T2:KEYS], start=True,
                                 stop=True).then_inc(max_ps, 1)

            def scores(j, g):
                b, h = divmod(j, HEADS)
                if g == 0:
                    pe.wait_ge(shift_done, j + 1)
                if j >= 1:
                    pe.wait_ge(exp_done, 2 * (j - 1) + g + 1)
                h = place(h)
                dst = span(2 + 2 * g, 3 * T1)
                queries = slice(b * T1, (b + 1) * T1)
                for n in range(3):
                    t = 3 * g + n
                    keys = slice(t * P, (t + 1) * P)
                    cols = slice(n * T1, (n + 1) * T1)
                    nc.tensor.matmul(dst[:, cols], k_a[:, h, keys], q_a[:, h, queries], start=True, stop=False)
                    last = nc.tensor.matmul(dst[:, cols], k_b[0:DH + 1, h, keys], q_b[0:DH + 1, h, queries],
                                            start=False, stop=True)
                last.then_inc(score_ps, 1)

            def bank7_free(use):
                n = MISC[use]
                shifts = shifts_before(n)
                if shifts > 0:
                    pe.wait_ge(shift_done, shifts)
                if n - shifts > 0:
                    pe.wait_ge(misc_done, n - shifts)

            def shift_row(i):
                pe.wait_ge(shift_ready, i + 1)
                bank7_free(("shift", i))
                for q in range(QT):
                    last = nc.tensor.matmul(misc[DH:DH + 1, q * P:(q + 1) * P], shift16[:, i, q:q + 1],
                                            ident16[:, :], start=True, stop=True)
                last.then_inc(misc_ps, 1)

            def values(j, q):
                b, h = divmod(j, HEADS)
                if q == 0:
                    pe.wait_ge(pl_done, pool_lo(j, 0))
                    if j >= 1:
                        pe.wait_ge(o_done, j)
                cols = slice(q * P, (q + 1) * P)
                for t in range(KT):
                    if q == 0 and t == KT // 2:
                        pe.wait_ge(pl_done, pool_lo(j, 1))
                        pe.wait_ge(pd_done, j + 1)
                    vh, vl = v_hi[:, b * KT + t, h, :], v_lo[:, b * KT + t, h, :]
                    ph, pl = p_hi[:, j % 3, t, cols], p_lo[:, j % 3, t, cols]
                    nc.tensor.matmul(o_ps[:, q, :], ph, vh, start=(t == 0), stop=False, skip_group_check=True)
                    nc.tensor.matmul(o_ps[:, q, 0:DH], ph, vl, start=False, stop=False, skip_group_check=True)
                    last = nc.tensor.matmul(o_ps[:, q, :], pl, vh, start=False, stop=(t == KT - 1),
                                            skip_group_check=True)
                last.then_inc(pv_ps, 1)

            def tail(b, s):
                bank7_free((s, b))
                if s in (TAIL_O0, TAIL_O1):
                    pe.wait_ge(o_done, HEADS * (b + 1))
                    for c in range(INNER // P):
                        last = nc.tensor.transpose(misc[:, c * P:(c + 1) * P],
                                                   o_sb[:, QT * b + s, c * P:(c + 1) * P], ident[:, :])
                elif s == TAIL_WO:
                    wait_split(pe, WO)
                    for q in range(QT):
                        t = QT * b + q
                        for c in range(INNER // P):
                            cols = slice(c * P, (c + 1) * P)
                            last = three(misc[:, q * D:(q + 1) * D], (oT[:, 0, t, cols], oT[:, 1, t, cols]),
                                         w_pair(WO, cols), start=(c == 0), stop=(c == INNER // P - 1))
                elif s == TAIL_X:
                    pe.wait_ge(xn_ready, NT + QT * (b + 1))
                    for q in range(QT):
                        last = nc.tensor.transpose(misc[:, q * P:(q + 1) * P], xn[:, QT * b + q, :], ident[:, :])
                elif s == TAIL_GATE:
                    pe.wait_ge(ld_rows, 96)
                    for q in range(QT):
                        at = b * T1 + q * P
                        last = nc.tensor.matmul(misc[:, q * E:(q + 1) * E], x2T[:, at:at + P], gw[:, :],
                                                start=True, stop=True)
                elif s == TAIL_COMB:
                    pe.wait_ge(comb_ready, b + 1)
                    for q in range(QT):
                        last = nc.tensor.transpose(misc[0:NE, q * P:(q + 1) * P], comb[:, QT * b + q, :],
                                                   ident[:, :])
                else:
                    for q in range(QT):
                        at = b * T1 + q * P
                        last = nc.tensor.matmul(misc[:, q * D:(q + 1) * D], combT[:, at:at + P], b2_rows[:, :],
                                                start=True, stop=True)
                last.then_inc(misc_ps, 1)

            for i in range(STEPS):
                k = i - FFN0
                if 0 <= k < NF:
                    b, e = k // NE, EORDER[k % NE]
                    if k == 0:
                        pe.wait_ge(max_done, QT * NH)
                    if k == 1:
                        pe.wait_ge(exp_done, 2 * NH)
                    if k >= 2:
                        pe.wait_ge(gelu_done, HC * (k - 1))
                    if k < EARLY:
                        pe.wait_ge(e_lo, k + 1)
                    elif k < NE:
                        pe.wait_ge(f_lo, k - EARLY + 1)
                    if k % NE == 0:
                        n = MISC[(TAIL_X, b)] + 1
                        pe.wait_ge(misc_done, n - shifts_before(n))
                    tok = slice(b * T1, (b + 1) * T1)
                    for c in range(HC):
                        cols = slice(c * P, (c + 1) * P)
                        last = three(span(2 * (k % 2), HC * T1)[:, c * T1:(c + 1) * T1],
                                     (wf[:, 0, e, 0, cols], wf[:, 1, e, 0, cols]),
                                     (x2h[:, 0, tok], x2h[:, 1, tok]))
                        if c % 2 == 1:
                            last.then_inc(h_ps, 1)
                if i < NH:
                    if i == ST_LAG:
                        read_out(before(late_items(i, 1)[0], 3))
                        keep_warm(WARM_STEP, 6)
                    if i == 0:
                        read_out(before(NI, 0))
                        pe.wait_ge(consts, 8)
                    max_scores(i, 0)
                if 0 <= i - ST_LAG < NH:
                    if i == ST_LAG:
                        read_out(before(NI, 1))
                    scores(i - ST_LAG, 0)
                if 0 <= i - PV_LAG < NH:
                    if i == PV_LAG:
                        read_out(NI)
                    values(i - PV_LAG, 0)
                for n in late_items(i, 0):
                    item_of(n)
                if i < NH:
                    max_scores(i, 1)
                if 1 <= i <= NH:
                    if i == 1:
                        read_out(before(NI - LATE, 3))
                    shift_row(i - 1)
                for n in late_items(i, 1):
                    item_of(n)
                if 0 <= i - ST_LAG < NH:
                    if i == ST_LAG:
                        read_out(before(NI, 2))
                    scores(i - ST_LAG, 1)
                if 0 <= i - PV_LAG < NH:
                    values(i - PV_LAG, 1)
                k = i - FFN0 - 2
                if 0 <= k < NF:
                    e = EORDER[k % NE]
                    pe.wait_ge(hl_done, k + 1)
                    if k >= 2:
                        pe.wait_ge(y_done, QT * (k - 1))
                    for q in range(QT):
                        for c in range(HC):
                            if q == 0 and c == HC // 2 and k in SHARED_LO:
                                pe.wait_ge(hd_done, shared(k) + 1)
                            at = c * T1 + q * P
                            cols = slice(c * P, (c + 1) * P)
                            last = three(banks[:, 4 + k % 2, q * D:(q + 1) * D],
                                         (hid_hi[:, k % HB, at:at + P], hid_lo[:, k % HB, at:at + P]),
                                         (wf[:, 0, e, 1, cols], wf[:, 1, e, 1, cols]),
                                         start=(c == 0), stop=(c == HC - 1))
                    last.then_inc(y_ps, 1)
                if i == BIAS_STEP:
                    pe.wait_ge(ld_rows, 96)
                    bank7_free(("b1", 0))
                    nc.tensor.transpose(misc[:, 0:NE * HC], b1_rows[:, :],
                                        ident[0:NE * HC, 0:NE * HC]).then_inc(misc_ps, 1)
                for b, s in tail_of(i):
                    tail(b, s)


_INS = ['x', 'ctx_1024', 'g_xattn', 'g_ffn', 'L0_xattn_Wq1', 'L0_xattn_Wk1', 'L0_xattn_Wv1', 'L0_xattn_Wk2',
        'L0_xattn_Wv2', 'L0_xattn_Wo', 'L0_xattn_bo', 'L0_ffn_gate_w', 'L0_ffn_gate_b', 'L0_ffn_w1', 'L0_ffn_b1',
        'L0_ffn_w2', 'L0_ffn_b2', 'L0_ffn_ws1', 'L0_ffn_bs1', 'L0_ffn_ws2', 'L0_ffn_bs2']
_OUTS = [((B, T1, D), 'float32')]


def kernel(**inputs):
    import numpy as _np
    import concourse.bacc as _bacc
    from concourse import mybir as _mybir
    from concourse.bass_utils import run_bass_kernel_spmd as _run

    nc = _bacc.Bacc("TRN2", target_bir_lowering=False, num_devices=1)
    arrays, args = {}, []
    for name in _INS:
        a = _np.ascontiguousarray(inputs[name])
        arrays[f"in_{name}_dram"] = a
        args.append(nc.dram_tensor(f"in_{name}_dram", a.shape, _mybir.dt.from_np(a.dtype), kind="ExternalInput").ap())
    for i, (shape, dtype) in enumerate(_OUTS):
        dt = _mybir.dt.from_np(_np.dtype(dtype))
        args.append(nc.dram_tensor(f"out_{i}_dram", shape, dt, kind="ExternalOutput").ap())
    block_kernel(nc, *args)
    r = _run(nc, [arrays], core_ids=[0])
    got = tuple(r.results[0][f"out_{i}_dram"] for i in range(len(_OUTS)))
    return got[0]
```
